# Optimizing a Trainium2 kernel written in Bass

```python
import numpy as np
import jax
import jax.numpy as jnp

def _softmax(x, axis=-1):
    return jax.nn.softmax(x, axis=axis)

def _gelu(x):
    return jax.nn.gelu(x, approximate=True)

def _silu(x):
    return jax.nn.silu(x)

def _sigmoid(x):
    return jax.nn.sigmoid(x)

def _layernorm(x, axis=-1, eps=1e-05):
    m = jnp.mean(x, axis=axis, keepdims=True)
    v = jnp.var(x, axis=axis, keepdims=True)
    return (x - m) / jnp.sqrt(v + eps)

def _scatter_add(tgt, idx, src, axis=0):
    return tgt.at[idx].add(src)

def _segment_sum(src, seg, n):
    return jax.ops.segment_sum(src, seg, n)
kernel_name = 'mk_decoder_postln_d1_seqx_r8_ccca5e'

def setup_inputs(seed: int=0):
    np.random.seed(seed)
    _w = jnp.asarray

    def _rec_inputs():
        import jax
        import jax.numpy as jnp
        _rk = jax.random.key(seed)
        x = -0.0002928 + 1 * jax.random.normal(jax.random.fold_in(_rk, 1), (8, 128, 256), jnp.float32)
        _lenS = 128 - jax.random.randint(jax.random.fold_in(_rk, 7), (8,), 0, max(1, 128 // 4) + 1, jnp.int32)
        _lenS2 = 128 - jax.random.randint(jax.random.fold_in(_rk, 8), (8,), 0, max(1, 128 // 4) + 1, jnp.int32)
        fside_S2_0 = -0.00337071 + 1.01897 * jax.random.normal(jax.random.fold_in(_rk, 11), (128,), jnp.float32)
        _ctx_2048P = jax.random.normal(jax.random.fold_in(_rk, 12), (8, 16, 256), jnp.float32)
        _ctx_2048c = jax.random.dirichlet(jax.random.fold_in(_rk, 512), 0.3 * jnp.ones((16,), jnp.float32), (8, 128))
        _ctx_2048t = jnp.einsum('bsk,bkd->bsd', _ctx_2048c, _ctx_2048P)
        _ctx_2048t = _ctx_2048t * jax.lax.rsqrt(jnp.mean(jnp.square(_ctx_2048t)) + 1e-12) * 0.953939
        ctx_2048 = 0.000675642 + 1.00031 * (_ctx_2048t + 0.3 * jax.random.normal(jax.random.fold_in(_rk, 612), (8, 128, 256), jnp.float32))
        return (x, fside_S2_0, ctx_2048)
    x, fside_S2_0, ctx_2048 = _rec_inputs()

    def _L0_attn_setup():
        import jax, jax.numpy as jnp
        import numpy as np
        DIM = 256
        HEADS = 16
        HEAD_DIM = DIM // HEADS
        RANK = 16
        ALPHA = 8.0
        SCALING = ALPHA / RANK
        SCALE = HEAD_DIM ** (-0.5)

        def lora_linear(x, W, b, Bm, Am):
            out = jnp.einsum('bld,od->blo', x, W) + b
            upd = jnp.einsum('blr,or->blo', jnp.einsum('bld,rd->blr', x, Bm), Am)
            return out + SCALING * upd

        def _split(t):
            B, L, D = t.shape
            return t.reshape(B, L, HEADS, HEAD_DIM).transpose(0, 2, 1, 3)
        key = jax.random.key(seed)
        ks = jax.random.split(key, 20)
        B, L = (4, 256)
        x = jax.random.normal(ks[0], (B, L, DIM), dtype=jnp.float32)
        s = 0.02
        inp = {'x': x}
        for i, name in enumerate(['q', 'k', 'v', 'o']):
            inp[f'W{name}'] = jax.random.normal(ks[1 + 4 * i], (DIM, DIM), jnp.float32) * s
            inp[f'b{name}'] = jax.random.normal(ks[2 + 4 * i], (DIM,), jnp.float32) * s
            inp[f'B{name}'] = jax.random.normal(ks[3 + 4 * i], (RANK, DIM), jnp.float32) * s
            inp[f'A{name}'] = jax.random.uniform(ks[4 + 4 * i], (DIM, RANK), jnp.float32, -0.1, 0.1)
        return inp
    _L0_attn_all = _L0_attn_setup()
    _L0_attn_in = {k: v for k, v in _L0_attn_all.items() if k in ('Wq', 'bq', 'Bq', 'Aq', 'Wk', 'bk', 'Bk', 'Ak', 'Wv', 'bv', 'Bv', 'Av', 'Wo', 'bo', 'Bo', 'Ao')}
    del _L0_attn_all

    def _L0_xattn_setup():
        import jax, jax.numpy as jnp
        import numpy as np
        key = jax.random.key(seed)
        ks = jax.random.split(key, 5)
        B, D, L, NH = (2, 128, 256, 8)
        H = D // NH
        return {'v': jax.random.normal(ks[0], (B, D, L), jnp.float32), 'k': jax.random.normal(ks[1], (H, L), jnp.float32) * 0.1, 'bias': jax.random.normal(ks[2], (D,), jnp.float32), 'x1': jax.random.normal(ks[3], (B, D, L), jnp.float32), 'x2': jax.random.normal(ks[4], (B, D, L), jnp.float32), 'num_heads': NH}
    _L0_xattn_all = _L0_xattn_setup()
    _L0_xattn_in = {k: v for k, v in _L0_xattn_all.items() if k in ('k',)}
    del _L0_xattn_all

    def _L0_ffn_setup():
        import jax, jax.numpy as jnp
        import numpy as np
        TOP_K = 4
        key = jax.random.key(seed)
        k1, k2, k3, k4 = jax.random.split(key, 4)
        B, S, D, E, H, O = (4, 256, 256, 8, 128, 256)
        scale = 0.02
        return {'x': jax.random.normal(k1, (B, S, D), dtype=jnp.float32), 'wg': jax.random.normal(k2, (D, E), dtype=jnp.float32) * scale, 'w1': jax.random.normal(k3, (E, H, D), dtype=jnp.float32) * scale, 'w2': jax.random.normal(k4, (E, O, H), dtype=jnp.float32) * scale}
    _L0_ffn_all = _L0_ffn_setup()
    _L0_ffn_in = {k: v for k, v in _L0_ffn_all.items() if k in ('wg', 'w1', 'w2')}
    del _L0_ffn_all
    return {'x': x, 'fside_S2_0': fside_S2_0, 'ctx_2048': ctx_2048, 'L0_attn_Wq': _L0_attn_in['Wq'], 'L0_attn_bq': _L0_attn_in['bq'], 'L0_attn_Bq': _L0_attn_in['Bq'], 'L0_attn_Aq': _L0_attn_in['Aq'], 'L0_attn_Wk': _L0_attn_in['Wk'], 'L0_attn_bk': _L0_attn_in['bk'], 'L0_attn_Bk': _L0_attn_in['Bk'], 'L0_attn_Ak': _L0_attn_in['Ak'], 'L0_attn_Wv': _L0_attn_in['Wv'], 'L0_attn_bv': _L0_attn_in['bv'], 'L0_attn_Bv': _L0_attn_in['Bv'], 'L0_attn_Av': _L0_attn_in['Av'], 'L0_attn_Wo': _L0_attn_in['Wo'], 'L0_attn_bo': _L0_attn_in['bo'], 'L0_attn_Bo': _L0_attn_in['Bo'], 'L0_attn_Ao': _L0_attn_in['Ao'], 'L0_xattn_k': _L0_xattn_in['k'], 'L0_ffn_wg': _L0_ffn_in['wg'], 'L0_ffn_w1': _L0_ffn_in['w1'], 'L0_ffn_w2': _L0_ffn_in['w2']}

def reference(x, fside_S2_0, ctx_2048, L0_attn_Wq, L0_attn_bq, L0_attn_Bq, L0_attn_Aq, L0_attn_Wk, L0_attn_bk, L0_attn_Bk, L0_attn_Ak, L0_attn_Wv, L0_attn_bv, L0_attn_Bv, L0_attn_Av, L0_attn_Wo, L0_attn_bo, L0_attn_Bo, L0_attn_Ao, L0_xattn_k, L0_ffn_wg, L0_ffn_w1, L0_ffn_w2):
    import jax
    import jax.numpy as jnp

    def _L0_attn_ref(x, Wq, bq, Bq, Aq, Wk, bk, Bk, Ak, Wv, bv, Bv, Av, Wo, bo, Bo, Ao):
        import jax, jax.numpy as jnp
        import numpy as np
        DIM = 256
        HEADS = 16
        HEAD_DIM = DIM // HEADS
        RANK = 16
        ALPHA = 8.0
        SCALING = ALPHA / RANK
        SCALE = HEAD_DIM ** (-0.5)

        def lora_linear(x, W, b, Bm, Am):
            out = jnp.einsum('bld,od->blo', x, W) + b
            upd = jnp.einsum('blr,or->blo', jnp.einsum('bld,rd->blr', x, Bm), Am)
            return out + SCALING * upd

        def _split(t):
            B, L, D = t.shape
            return t.reshape(B, L, HEADS, HEAD_DIM).transpose(0, 2, 1, 3)
        q = _split(lora_linear(x, Wq, bq, Bq, Aq))
        k = _split(lora_linear(x, Wk, bk, Bk, Ak))
        v = _split(lora_linear(x, Wv, bv, Bv, Av))
        scores = jnp.einsum('bhqd,bhkd->bhqk', q, k) * SCALE
        attn = jax.nn.softmax(scores, axis=-1)
        out = jnp.einsum('bhqk,bhkd->bhqd', attn, v)
        B, H, L, hd = out.shape
        out = out.transpose(0, 2, 1, 3).reshape(B, L, H * hd)
        return lora_linear(out, Wo, bo, Bo, Ao)

    def _L0_xattn_ref(v, k, bias, x1, x2, num_heads):
        import jax, jax.numpy as jnp
        import numpy as np
        B, D, L = v.shape
        H = D // num_heads
        fft_size = 2 * L
        vr = v.reshape(B, H, num_heads, L)
        x1r = x1.reshape(B, H, num_heads, L)
        x2r = x2.reshape(B, H, num_heads, L)
        kv = vr[:, :, :, None, :] * x2r[:, :, None, :, :]
        k_f = jnp.fft.rfft(k.astype(jnp.float32), n=fft_size)
        y = jnp.fft.irfft(jnp.fft.rfft(kv, n=fft_size) * k_f[None, :, None, None, :], n=fft_size)[..., :L]
        skip = bias.astype(jnp.float32).reshape(H, num_heads)[None, :, :, None, None]
        y = y + kv * skip
        out = jnp.einsum('bhijl,bhil->bhjl', y, x1r)
        return out.reshape(B, D, L)

    def _L0_ffn_ref(x, wg, w1, w2):
        import jax, jax.numpy as jnp
        import numpy as np
        TOP_K = 4
        B, S, D = x.shape
        xt = x.reshape(B * S, D)
        gate = xt @ wg
        top_val, top_idx = jax.lax.top_k(gate, TOP_K)
        gs = jax.nn.softmax(top_val, axis=-1)
        gs_eff = jnp.ones_like(gs) + gs - jax.lax.stop_gradient(gs)
        h = jax.nn.relu(jnp.einsum('nd,ehd->neh', xt, w1))
        out_all = jnp.einsum('neh,eoh->neo', h, w2)
        out_k = jnp.take_along_axis(out_all, top_idx[:, :, None], axis=1)
        out = jnp.einsum('nk,nko->no', gs_eff, out_k)
        return out.reshape(B, S, -1)
    x = _layernorm(x + _L0_attn_ref(x, L0_attn_Wq, L0_attn_bq, L0_attn_Bq, L0_attn_Aq, L0_attn_Wk, L0_attn_bk, L0_attn_Bk, L0_attn_Ak, L0_attn_Wv, L0_attn_bv, L0_attn_Bv, L0_attn_Av, L0_attn_Wo, L0_attn_bo, L0_attn_Bo, L0_attn_Ao), axis=-1)
    x = _layernorm(x + _L0_xattn_ref(x, L0_xattn_k, fside_S2_0, ctx_2048, ctx_2048, 8), axis=-1)
    x = _layernorm(x + _L0_ffn_ref(x, L0_ffn_wg, L0_ffn_w1, L0_ffn_w2), axis=-1)
    return x

_drawn_inputs = setup_inputs


def setup_inputs(seed=0):
    import zlib

    import numpy as np

    out = dict(_drawn_inputs(seed))
    spreads = {}
    factors = {'L0_attn_Wq': 8.0,
     'L0_attn_bq': 8.0,
     'L0_attn_Bq': 8.0,
     'L0_attn_Aq': 8.0,
     'L0_attn_Wk': 8.0,
     'L0_attn_bk': 64.0,
     'L0_attn_Bk': 8.0,
     'L0_attn_Ak': 8.0,
     'L0_attn_Wv': 3.843,
     'L0_attn_bv': 5.07,
     'L0_attn_Bv': 8.0,
     'L0_attn_Av': 8.0,
     'L0_attn_Wo': 3.286,
     'L0_attn_Bo': 8.0,
     'L0_attn_Ao': 8.0,
     'L0_attn_bo': 8.0}
    for name, (base, spread) in spreads.items():
        noise = np.random.default_rng([zlib.crc32(name.encode()), seed]).standard_normal(out[name].shape)
        drawn = base * np.exp(spread * noise) if base else spread * noise
        out[name] = jnp.asarray(drawn.astype(out[name].dtype))
    for name, factor in factors.items():
        out[name] = (out[name] * factor).astype(out[name].dtype)
    return out
```

```python
from contextlib import ExitStack

import concourse.bass as bass
from concourse import mybir

F32 = mybir.dt.float32
I32 = mybir.dt.int32
ALU = mybir.AluOpType
ACT = mybir.ActivationFunctionType
AX = mybir.AxisListType

B = 8
S = 128
D = 256
C = D // 128
HEADS, HD = 16, 16
GROUPS = 4
GH = HEADS // GROUPS
RANK = 16
LORA = 8.0 / RANK
SCALE = HD ** -0.5
NH = 16
CH = S // NH
E, TOP, HID = 8, 4, 128
EPS = 1e-5
NEWTON = 3
NEWTON_OPS = 4 + 3 * NEWTON
MATS = 4
Q, K, V, O = range(MATS)
TOEP_SLOTS = 4
IDENT, BLOCK, HMASK, TRI, CONSTS = 0, 128, 256, 264, 328


def program(nc, x, xT, ctx_rows, ctx_cols, WT, loraB, loraA, bqk, bvo, skip_bias, toep, w1T, w2T, wgT, consts, out):
    with ExitStack() as stack:
        def sb(name, shape, dt=F32):
            return stack.enter_context(nc.sbuf_tensor(name, shape, dt))

        def sem(name):
            return stack.enter_context(nc.semaphore(name))

        x_sb = sb("x_sb", [S, B, D])
        xT_sb = sb("xT_sb", [128, 2, C, S])
        ctx_r = sb("ctx_r", [S, B, D])
        ctx_c = sb("ctx_c", [128, C, B, S])
        w_sb = sb("w_sb", [128, MATS, C, D])
        loraB_sb = sb("loraB_sb", [RANK, MATS, D])
        loraA_sb = sb("loraA_sb", [RANK, MATS, D])
        bqk_sb = sb("bqk_sb", [128, 2, C])
        bvo_sb = sb("bvo_sb", [128, 2, D])
        skip_sb = sb("skip_sb", [128, 1])
        toep_sb = sb("toep_sb", [128, TOEP_SLOTS, 2, 128])
        w1_sb = sb("w1_sb", [128, C, E * HID])
        w2_sb = sb("w2_sb", [HID, E, D])
        wg_sb = sb("wg_sb", [128, C, E])
        const_sb = sb("const_sb", [128, CONSTS])
        ident = const_sb[:, IDENT:IDENT + 128]
        block_ones = const_sb[:, BLOCK:BLOCK + 128]
        head_mask = const_sb[:, HMASK:HMASK + 8].rearrange("p (e w) -> p e w", e=2)
        earlier = const_sb[:, TRI:TRI + E * E]
        qT = sb("qT", [128, 2, C, S])
        kT = sb("kT", [128, 2, C, S])
        kM = sb("kM", [128, 2, C, 2, GH, S])
        vz = sb("vz", [S, 2, C, 2, GH, 2 * HD])
        rowmax = sb("rowmax", [S, 2, GH])
        shifted = sb("shifted", [S, 2, GH * S])
        probs = sb("probs", [S, 2, GH * S])
        probsT = sb("probsT", [S, 2, GH * S])
        ones = sb("ones", [128, 2, 2 * HD])
        inv_sum = sb("inv_sum", [128, C, S])
        attnT = sb("attnT", [128, C, S])
        x1 = sb("x1", [S, B, D])
        x2 = sb("x2", [S, B, D])
        stats = sb("stats", [S, B, 6])
        moments = sb("moments", [S, B, 2])
        nw_v = sb("nw_v", [S, B])
        nw_h = sb("nw_h", [S, B])
        nw_a = sb("nw_a", [S, B])
        rstd = sb("rstd", [S, B])
        vT = sb("vT", [128, C, B, S])
        gated = sb("gated", [S, B, D])
        direct = sb("direct", [S, B, D])
        kv = sb("kv", [128, 2, C, B * CH * CH])
        z = sb("z", [128, 2, C, B * CH * CH])
        mixT = sb("mixT", [128, C, B, S])
        x2T = sb("x2T", [128, C, B * S])
        gateT = sb("gateT", [E, B * S])
        gate = sb("gate", [S, B, E])
        above = sb("above", [S, B, E * E])
        ties = sb("ties", [S, B, E * E])
        rank = sb("rank", [S, B, E])
        chosen = sb("chosen", [S, B, E])
        top = sb("top", [S, B])
        soft = sb("soft", [S, B, E])
        total = sb("total", [S, B])
        weight = sb("weight", [S, B, E])
        hT = sb("hT", [HID, 2, 2 * S])
        final = sb("final", [S, B, D])

        bank = [stack.enter_context(nc.psum_tensor(f"bank{i}", [128, 512], F32)) for i in range(8)]
        ps_scores, ps_turned = bank[0:2], bank[2:4]
        ps_attn, ps_qk, ps_v, ps_o = bank[4], bank[5], bank[6], bank[7]

        ld_w, ld_lora, ld_small, ld_const = sem("ld_w"), sem("ld_lora"), sem("ld_small"), sem("ld_const")
        ld_x, ld_ctx, ld_ffn = sem("ld_x"), sem("ld_ctx"), sem("ld_ffn")
        ld_xT = [sem("ld_xT0"), sem("ld_xT1")]
        ld_toep = [sem(f"ld_toep{i}") for i in range(TOEP_SLOTS)]
        stored = sem("stored")
        lora_done, w_ready, cleared, xb_ready = sem("lora_done"), sem("w_ready"), sem("cleared"), sem("xb_ready")
        qk_done, v_done, qk_ready, v_ready, kM_ready = (
            sem("qk_done"), sem("v_done"), sem("qk_ready"), sem("v_ready"), sem("kM_ready"))
        scores_done, max_ready, shifted_ready, probs_ready, turned_done, probsT_ready = (
            sem("scores_done"), sem("max_ready"), sem("shifted_ready"), sem("probs_ready"), sem("turned_done"),
            sem("probsT_ready"))
        pv_done, inv_ready, attnT_ready, o_done = sem("pv_done"), sem("inv_ready"), sem("attnT_ready"), sem("o_done")
        x1_summed, x1_stats, x1_moments, x1_ready = (
            sem("x1_summed"), sem("x1_stats"), sem("x1_moments"), sem("x1_ready"))
        newton = sem("newton")
        vT_done, vT_ready, gated_ready, blocks_done, direct_ready, base_ready = (
            sem("vT_done"), sem("vT_ready"), sem("gated_ready"), sem("blocks_done"), sem("direct_ready"),
            sem("base_ready"))
        kv_ready, conv_done, z_ready, mixT_ready = sem("kv_ready"), sem("conv_done"), sem("z_ready"), sem("mixT_ready")
        mix_done, x2_summed, x2_stats, x2_moments, x2_ready = (
            sem("mix_done"), sem("x2_summed"), sem("x2_stats"), sem("x2_moments"), sem("x2_ready"))
        x2T_done, x2T_ready, gateT_done, gateT_ready, gate_done, gating, gate_exp = (
            sem("x2T_done"), sem("x2T_ready"), sem("gateT_done"), sem("gateT_ready"), sem("gate_done"),
            sem("gating"), sem("gate_exp"))
        h_done, h_ready, expert_done, combined = sem("h_done"), sem("h_ready"), sem("expert_done"), sem("combined")
        x3_stats, x3_moments, final_ready = sem("x3_stats"), sem("x3_moments"), sem("final_ready")

        block = stack.enter_context(nc.Block())

        @block.sync
        def _(sp):
            sp.dma_start(loraB_sb[:], loraB).then_inc(ld_lora, 16)
            sp.dma_start(loraA_sb[:], loraA).then_inc(ld_lora, 16)
            sp.dma_start(w_sb[:], WT).then_inc(ld_w, 16)
            sp.dma_start(xT_sb[:, 0], xT[0]).then_inc(ld_xT[0], 16)
            sp.dma_start(const_sb[:], consts).then_inc(ld_const, 16)
            sp.dma_start(xT_sb[:, 1], xT[1]).then_inc(ld_xT[1], 16)
            sp.dma_start(x_sb[:], x.rearrange("b s d -> s b d")).then_inc(ld_x, 16)
            for h in range(TOEP_SLOTS):
                sp.dma_start(toep_sb[:, h], toep[h]).then_inc(ld_toep[h], 16)
            sp.dma_start(ctx_r[:], ctx_rows.rearrange("b s d -> s b d")).then_inc(ld_ctx, 16)
            sp.dma_start(ctx_c[:], ctx_cols).then_inc(ld_ctx, 16)
            sp.dma_start(w1_sb[:], w1T).then_inc(ld_ffn, 16)
            sp.dma_start(w2_sb[:], w2T).then_inc(ld_ffn, 16)
            sp.dma_start(wg_sb[:], wgT).then_inc(ld_ffn, 16)
            with sp.Fori(2, B - 1, 2) as i:
                for slot in range(2):
                    sp.wait_ge(v_done, i + slot - 1)
                    sp.dma_start(xT_sb[:, slot], xT[bass.ds(i + slot, 1)].rearrange("o p c s -> (o p) c s")
                                 ).then_inc(ld_xT[slot], 16)
            with sp.Fori(TOEP_SLOTS, NH - TOEP_SLOTS + 1, TOEP_SLOTS) as i:
                for slot in range(TOEP_SLOTS):
                    sp.wait_ge(conv_done, 2 * (i + slot - TOEP_SLOTS) + 2)
                    sp.dma_start(toep_sb[:, slot], toep[bass.ds(i + slot, 1)].rearrange("o p k m -> (o p) k m")
                                 ).then_inc(ld_toep[slot], 16)
            with sp.Fori(0, B) as b:
                sp.wait_ge(final_ready, b + 1)
                sp.dma_start(out[bass.ds(b, 1)].rearrange("o s d -> (o s) d"),
                             final[:, bass.ds(b, 1), :].rearrange("s o d -> s (o d)")).then_inc(stored, 16)
            sp.wait_ge(stored, 16 * B)

        @block.scalar
        def _(act):
            act.dma_start(bqk_sb[:], bqk).then_inc(ld_small, 16)
            act.dma_start(bvo_sb[:], bvo.partition_broadcast(128)).then_inc(ld_small, 16)
            act.dma_start(skip_sb[:], skip_bias).then_inc(ld_small, 16)

            def qk_out(b, slot):
                act.wait_ge(qk_done, b + 1)
                for c in range(C):
                    for m, buf in ((Q, qT), (K, kT)):
                        nc.scalar.activation(buf[:, slot, c], ps_qk[:, (2 * c + m) * S:(2 * c + m + 1) * S],
                                             ACT.Identity, bias=bqk_sb[:, m, c:c + 1]).then_inc(qk_ready, 1)

            def exp(G, par, first=False):
                act.wait_ge(shifted_ready, G + 1)
                if not first:
                    act.wait_ge(turned_done, G - 1)
                nc.scalar.activation(probs[:, par], shifted[:, par], ACT.Exp, scale=SCALE).then_inc(probs_ready, 1)

            def turned_out(G, par, first=False):
                act.wait_ge(turned_done, G + 1)
                if not first:
                    act.wait_ge(pv_done, G - 1)
                nc.scalar.copy(probsT[:, par], ps_turned[par][:]).then_inc(probsT_ready, 1)

            def step(b, slot, first=False, last=False):
                for g in range(GROUPS):
                    G = GROUPS * b + g
                    exp(G, g % 2, first and g < 2)
                    if g == 0 and not last:
                        if not first:
                            act.wait_ge(scores_done, GROUPS * b)
                            act.wait_ge(kM_ready, 4 * b)
                        qk_out(b + 1, 1 - slot)
                    turned_out(G, g % 2, first and g < 2)

            act.wait_ge(ld_small, 48)
            qk_out(0, 0)
            step(0, 0, first=True)
            with act.Fori(1, B - 2, 2) as i:
                step(i, 1)
                step(i + 1, 0)
            step(B - 1, 1, last=True)

            for b2 in range(B // 2):
                act.wait_ge(vT_done, b2 + 1)
                nc.scalar.copy(vT[:, :, 2 * b2:2 * b2 + 2, :],
                               bank[b2 % 4][:].rearrange("p (b c s) -> p c b s", b=2, c=C)).then_inc(vT_ready, 1)
            for b2 in range(B // 2):
                act.wait_ge(x2T_done, b2 + 1)
                nc.scalar.copy(x2T[:].rearrange("p c (b s) -> p c b s", b=B)[:, :, 2 * b2:2 * b2 + 2, :],
                               bank[4 + b2 % 2][:].rearrange("p (b c s) -> p c b s", b=2, c=C)).then_inc(x2T_ready, 1)
            for n in range(2):
                act.wait_ge(gateT_done, n + 1)
                nc.scalar.copy(gateT[:, n * 512:(n + 1) * 512], bank[6 + n][0:E, :]).then_inc(gateT_ready, 1)

            def relu(k, slot, first=False):
                act.wait_ge(h_done, k + 1)
                if not first:
                    act.wait_ge(expert_done, k - 1)
                nc.scalar.activation(hT[:, slot], bank[slot][:, 0:2 * S], ACT.Relu).then_inc(h_ready, 1)

            relu(0, 0, True)
            act.wait_ge(gating, GATE_SHIFTED)
            nc.scalar.activation(soft[:], soft[:], ACT.Exp).then_inc(gate_exp, 1)
            for e in range(1, E):
                relu(e, e % 2, e < 2)
            with act.Fori(1, B // 2) as p:
                for e in range(E):
                    relu(E * p + e, e % 2)

        @block.gpsimd
        def _(pool):
            nc.gpsimd.memset(ones[:], 0.0).then_inc(cleared, 1)
            nc.gpsimd.memset(vz[:], 0.0).then_inc(cleared, 1)
            pool.wait_ge(cleared, 1)
            nc.gpsimd.memset(ones[:, 0, 0:HD], 1.0).then_inc(cleared, 1)
            nc.gpsimd.memset(ones[:, 1, HD:2 * HD], 1.0).then_inc(cleared, 1)

            def mask_keys(b, slot):
                for c in range(C):
                    pool.wait_ge(qk_ready, 4 * b + 2 * c + 2)
                    for e in range(2):
                        nc.gpsimd.tensor_tensor(
                            kM[:, slot, c, e], kT[:, slot, c].unsqueeze(1).to_broadcast([128, GH, S]),
                            head_mask[:, e].unsqueeze(2).to_broadcast([128, GH, S]), ALU.mult).then_inc(kM_ready, 1)

            pool.wait_ge(ld_const, 16)
            mask_keys(0, 0)
            mask_keys(1, 1)
            pool.wait_ge(ld_x, 16)
            pool.wait_ge(ld_small, 48)
            nc.gpsimd.tensor_tensor(x_sb[:], x_sb[:], bvo_sb[:, 1].unsqueeze(1).to_broadcast([S, B, D]),
                                    ALU.add).then_inc(xb_ready, 1)
            with pool.Fori(2, B - 1, 2) as i:
                for slot in range(2):
                    pool.wait_ge(scores_done, GROUPS * (i + slot) - GROUPS)
                    mask_keys(i + slot, slot)

            def products(h, slot, first=False):
                if not first:
                    pool.wait_ge(conv_done, 2 * h - 2)
                for c in range(C):
                    nc.gpsimd.tensor_tensor(
                        kv[:, slot, c].rearrange("p (b i j) -> p b i j", b=B, i=CH),
                        vT[:, c, :, bass.ds(CH * h, CH)].unsqueeze(3).to_broadcast([128, B, CH, CH]),
                        ctx_c[:, c, :, bass.ds(CH * h, CH)].unsqueeze(2).to_broadcast([128, B, CH, CH]),
                        ALU.mult).then_inc(kv_ready, 1)

            pool.wait_ge(ld_ctx, 32)
            pool.wait_ge(vT_ready, B // 2)
            products(0, 0, True)
            products(1, 1, True)
            with pool.Fori(2, NH - 5, 4) as i:
                for u in range(4):
                    products(i + u, u % 2)
            products(NH - 2, 0)
            products(NH - 1, 1)
            for b in range(B):
                pool.wait_ge(direct_ready, b + 1)
                nc.gpsimd.tensor_tensor(x1[:, b], x1[:, b], direct[:, b], ALU.add).then_inc(base_ready, 1)

        @block.vector
        def _(dve):
            def newton_rstd(n, done):
                cut = slice(0, n)
                v, hv, a, y = nw_v[:, cut], nw_h[:, cut], nw_a[:, cut], rstd[:, cut]
                var = moments[:, cut, 1]
                nc.vector.tensor_scalar(v, var, EPS, None, ALU.add).then_inc(newton, 1)
                dve.wait_ge(newton, done + 1)
                nc.vector.tensor_scalar(y.bitcast(I32), v.bitcast(I32), 1, None, ALU.arith_shift_right).then_inc(newton, 1)
                nc.vector.tensor_scalar(hv, v, -0.5, None, ALU.mult).then_inc(newton, 1)
                dve.wait_ge(newton, done + 3)
                nc.vector.tensor_scalar(y.bitcast(I32), y.bitcast(I32), -1.0, float(0x5F3759DF), ALU.mult,
                                        ALU.add).then_inc(newton, 1)
                for k in range(NEWTON):
                    at = done + 4 + 3 * k
                    dve.wait_ge(newton, at)
                    nc.vector.tensor_tensor(a, y, y, ALU.mult).then_inc(newton, 1)
                    dve.wait_ge(newton, at + 1)
                    nc.vector.tensor_tensor(a, a, hv, ALU.mult).then_inc(newton, 1)
                    dve.wait_ge(newton, at + 2)
                    nc.vector.scalar_tensor_tensor(out=y, in0=a, scalar=1.5, in1=y, op0=ALU.add,
                                                   op1=ALU.mult).then_inc(newton, 1)
                dve.wait_ge(newton, done + NEWTON_OPS)

            dve.wait_ge(ld_w, 16)
            for m in range(MATS):
                dve.wait_ge(lora_done, m + 1)
                nc.vector.scalar_tensor_tensor(
                    out=w_sb[:, m].rearrange("p c d -> p (c d)"), in0=bank[m][:], scalar=LORA,
                    in1=w_sb[:, m].rearrange("p c d -> p (c d)"), op0=ALU.mult, op1=ALU.add).then_inc(w_ready, 1)

            def v_out(b, slot):
                dve.wait_ge(v_done, b + 1)
                for e in range(2):
                    cut = lambda t: t.rearrange("p (c w e d) -> p c w e d", c=C, w=GH, e=2)[:, :, :, e, :]
                    nc.vector.tensor_tensor(vz[:, slot, :, e, :, HD * e:HD * (e + 1)], cut(ps_v[:, 0:D]),
                                            cut(bvo_sb[:, 0]), ALU.add).then_inc(v_ready, 1)

            def shift(G, par, first=False):
                dve.wait_ge(scores_done, G + 1)
                scores = ps_scores[par][:].rearrange("p (h k) -> p h k", h=GH)
                nc.vector.tensor_reduce(rowmax[:, par], scores, AX.X, ALU.max).then_inc(max_ready, 1)
                dve.wait_ge(max_ready, G + 1)
                if not first:
                    dve.wait_ge(probs_ready, G - 1)
                nc.vector.tensor_tensor(shifted[:, par].rearrange("p (h k) -> p h k", h=GH), scores,
                                        rowmax[:, par].unsqueeze(2).to_broadcast([S, GH, S]),
                                        ALU.subtract).then_inc(shifted_ready, 1)

            def normalise(b):
                dve.wait_ge(pv_done, GROUPS * b + GROUPS)
                nc.vector.reciprocal(inv_sum[:].rearrange("p c s -> p (c s)"), ps_attn[:, D:2 * D]).then_inc(inv_ready, 1)
                dve.wait_ge(inv_ready, b + 1)
                nc.vector.tensor_tensor(attnT[:].rearrange("p c s -> p (c s)"), ps_attn[:, 0:D],
                                        inv_sum[:].rearrange("p c s -> p (c s)"), ALU.mult).then_inc(attnT_ready, 1)

            def residual(b):
                at = bass.ds(b, 1)
                one = lambda t: t[:, at, :].rearrange("p o d -> p (o d)")
                dve.wait_ge(o_done, b + 1)
                nc.vector.tensor_tensor(one(x1), ps_o[:, 0:D], one(x_sb), ALU.add).then_inc(x1_summed, 1)
                dve.drain()
                nc.vector.bn_stats(one(stats), one(x1)).then_inc(x1_stats, 1)

            def step(b, slot, first=False, last=False):
                G = GROUPS * b
                shift(G, 0, first)
                shift(G + 1, 1, first)
                if not first:
                    normalise(b - 1)
                shift(G + 2, 0)
                if not last:
                    v_out(b + 1, 1 - slot)
                shift(G + 3, 1)
                if not first:
                    residual(b - 1)

            dve.wait_ge(ld_small, 48)
            dve.wait_ge(cleared, 4)
            v_out(0, 0)
            step(0, 0, first=True)
            dve.wait_ge(xb_ready, 1)
            with dve.Fori(1, B - 2, 2) as i:
                step(i, 1)
                step(i + 1, 0)
            step(B - 1, 1, last=True)
            normalise(B - 1)
            residual(B - 1)

            dve.wait_ge(x1_stats, B)
            for b in range(B):
                nc.vector.bn_aggr(moments[:, b], stats[:, b]).then_inc(x1_moments, 1)
            dve.wait_ge(x1_moments, B)
            newton_rstd(B, 0)
            for b in range(B):
                nc.vector.tensor_scalar(x1[:, b], x1[:, b], moments[:, b, 0:1], rstd[:, b:b + 1], ALU.subtract,
                                        ALU.mult).then_inc(x1_ready, 1)
            dve.wait_ge(ld_ctx, 32)
            for b in range(B):
                dve.wait_ge(x1_ready, b + 1)
                nc.vector.scalar_tensor_tensor(out=gated[:, b], in0=x1[:, b], scalar=skip_sb[:, 0:1], in1=ctx_r[:, b],
                                               op0=ALU.mult, op1=ALU.mult).then_inc(gated_ready, 1)
            for b in range(B):
                if b % 2 == 0:
                    dve.wait_ge(blocks_done, b // 2 + 1)
                nc.vector.tensor_tensor(direct[:, b], bank[4 + b // 2][:, (b % 2) * D:(b % 2 + 1) * D], ctx_r[:, b],
                                        ALU.mult).then_inc(direct_ready, 1)

            def gather(h, par, first=False):
                if not first:
                    dve.wait_ge(mixT_ready, 2 * h - 2)
                for c in range(C):
                    dve.wait_ge(conv_done, 2 * h + c + 1)
                    nc.vector.tensor_tensor(
                        z[:, par, c].rearrange("p (b i j) -> p b i j", b=B, i=CH),
                        bank[2 * par + c][:].rearrange("p (b i j) -> p b i j", b=B, i=CH),
                        ctx_c[:, c, :, bass.ds(CH * h, CH)].unsqueeze(3).to_broadcast([128, B, CH, CH]),
                        ALU.mult).then_inc(z_ready, 1)
                for c in range(C):
                    dve.wait_ge(z_ready, 2 * h + c + 1)
                    nc.vector.tensor_reduce(mixT[:, c, :, bass.ds(CH * h, CH)],
                                            z[:, par, c].rearrange("p (b i j) -> p b j i", b=B, i=CH),
                                            AX.X, ALU.add).then_inc(mixT_ready, 1)

            gather(0, 0, True)
            gather(1, 1, True)
            with dve.Fori(2, NH - 1, 2) as i:
                for u in range(2):
                    gather(i + u, u)

            for b in range(B):
                dve.wait_ge(mix_done, b // 2 + 1)
                dve.wait_ge(base_ready, b + 1)
                nc.vector.tensor_tensor(x2[:, b], bank[4 + b // 2][:, (b % 2) * D:(b % 2 + 1) * D], x1[:, b],
                                        ALU.add).then_inc(x2_summed, 1)
                dve.wait_ge(x2_summed, b + 1)
                nc.vector.bn_stats(stats[:, b], x2[:, b]).then_inc(x2_stats, 1)
                dve.wait_ge(x2_stats, b + 1)
                nc.vector.bn_aggr(moments[:, b], stats[:, b]).then_inc(x2_moments, 1)
            dve.wait_ge(x2_moments, B)
            newton_rstd(B, NEWTON_OPS)
            for b in range(B):
                nc.vector.tensor_scalar(x2[:, b], x2[:, b], moments[:, b, 0:1], rstd[:, b:b + 1], ALU.subtract,
                                        ALU.mult).then_inc(x2_ready, 1)

            step_no = [0]

            def link(ins):
                step_no[0] += 1
                ins.then_inc(gating, 1)
                dve.wait_ge(gating, step_no[0])

            pair = [S, B, E, E]
            four = lambda t: t[:].rearrange("p b (e f) -> p b e f", e=E)
            dve.wait_ge(gate_done, 1)
            link(nc.vector.tensor_copy(gate[:].rearrange("p b e -> p (b e)"), bank[2][:, 0:B * E]))
            link(nc.vector.tensor_reduce(top[:], gate[:], AX.X, ALU.max))
            link(nc.vector.tensor_tensor(soft[:], gate[:], top[:].unsqueeze(2).to_broadcast([S, B, E]), ALU.subtract))
            assert step_no[0] == GATE_SHIFTED
            theirs = gate[:].unsqueeze(2).to_broadcast(pair)
            own = gate[:].unsqueeze(3).to_broadcast(pair)
            link(nc.vector.tensor_tensor(four(above), theirs, own, ALU.is_gt))
            link(nc.vector.tensor_tensor(four(ties), theirs, own, ALU.is_equal))
            link(nc.vector.tensor_tensor(ties[:], ties[:], earlier.unsqueeze(1).to_broadcast([S, B, E * E]), ALU.mult))
            link(nc.vector.tensor_tensor(above[:], above[:], ties[:], ALU.add))
            link(nc.vector.tensor_reduce(rank[:], four(above), AX.X, ALU.add))
            link(nc.vector.tensor_scalar(chosen[:], rank[:], float(TOP), None, ALU.is_lt))
            dve.wait_ge(gate_exp, 1)
            link(nc.vector.tensor_tensor(soft[:], soft[:], chosen[:], ALU.mult))
            link(nc.vector.tensor_reduce(total[:], soft[:], AX.X, ALU.add))
            link(nc.vector.reciprocal(total[:], total[:]))
            link(nc.vector.tensor_tensor(soft[:], soft[:], total[:].unsqueeze(2).to_broadcast([S, B, E]), ALU.mult))
            link(nc.vector.tensor_scalar(weight[:], soft[:], 1.0, None, ALU.add))
            link(nc.vector.tensor_tensor(weight[:], weight[:], soft[:], ALU.subtract))
            link(nc.vector.tensor_tensor(weight[:], weight[:], chosen[:], ALU.mult))

            def combine(p, e, first=False):
                k = E * p + e
                dve.wait_ge(expert_done, k + 1)
                for u in range(2):
                    if not first:
                        dve.wait_ge(combined, 2 * k + u - 1)
                    row = x2[:, bass.ds(2 * p + u, 1), :].rearrange("p o d -> p (o d)")
                    nc.vector.scalar_tensor_tensor(
                        out=row, in0=bank[4 + e % 2][:, u * D:(u + 1) * D],
                        scalar=weight[:, bass.ds(2 * p + u, 1), e:e + 1].rearrange("p o d -> p (o d)"), in1=row,
                        op0=ALU.mult, op1=ALU.add).then_inc(combined, 1)

            def finish(p):
                one = lambda t, u: t[:, bass.ds(2 * p + u, 1), :].rearrange("p o d -> p (o d)")
                for u in range(2):
                    dve.drain()
                    nc.vector.bn_stats(stats[:, u], one(x2, u)).then_inc(x3_stats, 1)
                    dve.drain()
                    nc.vector.bn_aggr(moments[:, u], stats[:, u]).then_inc(x3_moments, 1)
                dve.wait_ge(x3_moments, 2 * p + 2)
                newton_rstd(2, NEWTON_OPS * (p + 2))
                for u in range(2):
                    nc.vector.tensor_scalar(one(final, u), one(x2, u), moments[:, u, 0:1],
                                            rstd[:, u:u + 1], ALU.subtract, ALU.mult
                                            ).then_inc(final_ready, 1)

            for e in range(E):
                combine(0, e, e == 0)
            finish(0)
            with dve.Fori(1, B // 2) as p:
                for e in range(E):
                    combine(p, e)
                finish(p)

        @block.tensor
        def _(pe):
            mm = nc.tensor.matmul
            pe.wait_ge(ld_lora, 32)
            for m in range(MATS):
                for c in range(C):
                    last = mm(bank[m][:, c * D:(c + 1) * D], loraB_sb[:, m, c * 128:(c + 1) * 128], loraA_sb[:, m],
                              start=True, stop=True)
                last.then_inc(lora_done, 1)

            def project_qk(b, slot, first=False):
                pe.wait_ge(ld_xT[slot], 8 * (b - slot) + 16)
                if not first:
                    pe.wait_ge(qk_ready, 4 * b)
                for c in range(C):
                    for m in (Q, K):
                        at = 2 * c + m
                        for d in range(C):
                            last = mm(ps_qk[:, at * S:(at + 1) * S], w_sb[:, m, d, c * 128:(c + 1) * 128],
                                      xT_sb[:, slot, d], start=(d == 0), stop=(d == C - 1))
                last.then_inc(qk_done, 1)

            def project_v(b, slot, first=False):
                if not first:
                    pe.wait_ge(v_ready, 2 * b)
                for d in range(C):
                    last = mm(ps_v[:, 0:D], xT_sb[:, slot, d], w_sb[:, V, d], start=(d == 0), stop=(d == C - 1))
                last.then_inc(v_done, 1)

            def scores(b, g, slot, first=False):
                c, e = g // 2, g % 2
                if e == 0:
                    pe.wait_ge(qk_ready, 4 * b + 2 * c + 1)
                pe.wait_ge(kM_ready, 4 * b + 2 * c + e + 1)
                if not first:
                    pe.wait_ge(shifted_ready, GROUPS * b + g - 1)
                mm(ps_scores[e][:], qT[:, slot, c], kM[:, slot, c, e].rearrange("p w s -> p (w s)"), start=True,
                   stop=True).then_inc(scores_done, 1)

            def turn(G, par, first=False):
                pe.wait_ge(probs_ready, G + 1)
                if not first:
                    pe.wait_ge(probsT_ready, G - 1)
                for n in range(GH):
                    last = nc.tensor.transpose(ps_turned[par][:, n * S:(n + 1) * S], probs[:, par, n * S:(n + 1) * S], ident)
                last.then_inc(turned_done, 1)

            def weigh(b, g, slot, first=False):
                c, e = g // 2, g % 2
                G = GROUPS * b + g
                pe.wait_ge(probsT_ready, G + 1)
                if g == 0:
                    pe.wait_ge(v_ready, 2 * b + 2)
                    if not first:
                        pe.wait_ge(attnT_ready, b)
                for part in range(2):
                    for w in range(GH):
                        rows = slice(32 * w, 32 * w + 32)
                        lhsT = vz[:, slot, c, e, w] if part == 0 else ones[:, e]
                        last = mm(ps_attn[rows, part * D + c * S:part * D + (c + 1) * S], lhsT,
                                  probsT[:, e, w * S:(w + 1) * S], start=(g == 0 and part == 0),
                                  stop=(g == GROUPS - 1 and part == 1), skip_group_check=True)
                last.then_inc(pv_done, 1)

            def project_o(b, first=False):
                pe.wait_ge(attnT_ready, b + 1)
                if first:
                    pe.wait_ge(w_ready, MATS)
                else:
                    pe.wait_ge(x1_summed, b)
                for c in range(C):
                    last = mm(ps_o[:, 0:D], attnT[:, c], w_sb[:, O, c], start=(c == 0), stop=(c == C - 1))
                last.then_inc(o_done, 1)

            def step(b, slot, first=False, last=False):
                for g in range(GROUPS):
                    if g < GROUPS - 1:
                        scores(b, g + 1, slot, first and g == 0)
                    elif not last:
                        scores(b + 1, 0, 1 - slot)
                    if g == 0 and not last:
                        project_qk(b + 1, 1 - slot)
                    if g == 1 and not last:
                        project_v(b + 1, 1 - slot)
                    if g == 2 and not first:
                        project_o(b - 1, isinstance(b, int) and b == 1)
                    turn(GROUPS * b + g, g % 2, first and g < 2)
                    if g > 0:
                        weigh(b, g - 1, slot, first)
                    elif not first:
                        weigh(b - 1, GROUPS - 1, 1 - slot)

            pe.wait_ge(w_ready, K + 1)
            project_qk(0, 0, True)
            pe.wait_ge(w_ready, MATS)
            project_v(0, 0, True)
            pe.wait_ge(ld_const, 16)
            pe.wait_ge(cleared, 4)
            scores(0, 0, 0, True)
            step(0, 0, first=True)
            with pe.Fori(1, B - 2, 2) as i:
                step(i, 1)
                step(i + 1, 0)
            step(B - 1, 1, last=True)
            weigh(B - 1, GROUPS - 1, 1)
            project_o(B - 1)

            pe.wait_ge(probsT_ready, GROUPS * B)
            for b in range(B):
                pe.wait_ge(x1_ready, b + 1)
                for c in range(C):
                    at = (b % 2) * D + c * 128
                    last = nc.tensor.transpose(bank[b // 2][:, at:at + 128], x1[:, b, c * 128:(c + 1) * 128], ident)
                if b % 2:
                    last.then_inc(vT_done, 1)
            for b in range(B):
                pe.wait_ge(gated_ready, b + 1)
                last = mm(bank[4 + b // 2][:, (b % 2) * D:(b % 2 + 1) * D], block_ones, gated[:, b], start=True, stop=True)
                if b % 2:
                    last.then_inc(blocks_done, 1)

            def convolve(h, par, slot, first=False):
                pe.wait_ge(ld_toep[slot], 4 * (h - slot) + 16)
                pe.wait_ge(kv_ready, 2 * h + 2)
                if not first:
                    pe.wait_ge(z_ready, 2 * h - 2)
                near, far = toep_sb[:, slot, 0], toep_sb[:, slot, 1]
                mm(bank[2 * par][:], near, kv[:, par, 0], start=True, stop=True).then_inc(conv_done, 1)
                mm(bank[2 * par + 1][:], far, kv[:, par, 0], start=True, stop=False)
                mm(bank[2 * par + 1][:], near, kv[:, par, 1], start=False, stop=True).then_inc(conv_done, 1)

            pe.wait_ge(vT_ready, B // 2)
            convolve(0, 0, 0, True)
            convolve(1, 1, 1, True)
            with pe.Fori(2, NH - 5, TOEP_SLOTS) as i:
                for u in range(TOEP_SLOTS):
                    convolve(i + u, u % 2, (2 + u) % TOEP_SLOTS)
            convolve(NH - 2, 0, 2)
            convolve(NH - 1, 1, 3)

            pe.wait_ge(direct_ready, B)
            pe.wait_ge(mixT_ready, 2 * NH)
            for b in range(B):
                for c in range(C):
                    at = (b % 2) * D + c * 128
                    last = nc.tensor.transpose(bank[4 + b // 2][:, at:at + 128], mixT[:, c, b], ident)
                if b % 2:
                    last.then_inc(mix_done, 1)
            pe.wait_ge(x2_summed, B)
            for b in range(B):
                pe.wait_ge(x2_ready, b + 1)
                if b >= 4 and b % 2 == 0:
                    pe.wait_ge(x2T_ready, b // 2 - 1)
                for c in range(C):
                    at = (b % 2) * D + c * 128
                    last = nc.tensor.transpose(bank[4 + b // 2 % 2][:, at:at + 128], x2[:, b, c * 128:(c + 1) * 128], ident)
                if b % 2:
                    last.then_inc(x2T_done, 1)
            pe.wait_ge(ld_ffn, 48)
            for n in range(2):
                pe.wait_ge(x2T_ready, 2 * n + 2)
                for c in range(C):
                    last = mm(bank[6 + n][0:E, :], wg_sb[:, c], x2T[:, c, n * 512:(n + 1) * 512], start=(c == 0),
                              stop=(c == C - 1))
                last.then_inc(gateT_done, 1)

            def hidden(p, e, first=False):
                k = E * p + e
                if not first:
                    pe.wait_ge(h_ready, k - 1)
                for c in range(C):
                    last = mm(bank[e % 2][:, 0:2 * S], w1_sb[:, c, e * HID:(e + 1) * HID],
                              x2T[:, c, bass.ds(2 * S * p, 2 * S)], start=(c == 0), stop=(c == C - 1))
                last.then_inc(h_done, 1)

            def expert(p, e, first=False):
                k = E * p + e
                pe.wait_ge(h_ready, k + 1)
                if not first:
                    pe.wait_ge(combined, 2 * k - 2)
                for u in range(2):
                    last = mm(bank[4 + e % 2][:, u * D:(u + 1) * D], hT[:, e % 2, u * S:(u + 1) * S], w2_sb[:, e],
                              start=True, stop=True)
                last.then_inc(expert_done, 1)

            hidden(0, 0, True)
            pe.wait_ge(gateT_ready, 2)
            for b in range(B):
                last = nc.tensor.transpose(bank[2][:, b * E:(b + 1) * E], gateT[:, b * S:(b + 1) * S], ident[0:E, 0:E])
            last.then_inc(gate_done, 1)

            def pair_of_entries(p, first=False, last=False):
                for e in range(E):
                    if e < E - 1:
                        hidden(p, e + 1, first and e == 0)
                    elif not last:
                        hidden(p + 1, 0)
                    expert(p, e, first and e < 2)

            pair_of_entries(0, first=True)
            with pe.Fori(1, B // 2 - 1) as p:
                pair_of_entries(p)
            pair_of_entries(B // 2 - 1, last=True)


GATE_SHIFTED = 3


INS = ["x", "xT", "ctx_rows", "ctx_cols", "WT", "loraB", "loraA", "bqk", "bvo", "skip_bias", "toep", "w1T", "w2T",
       "wgT", "consts"]


def kernel(**inputs):
    import numpy as np
    import concourse.bacc as bacc
    from concourse.bass_utils import run_bass_kernel_spmd

    a = {k: np.asarray(v) for k, v in inputs.items()}
    x, ctx = a["x"], a["ctx_2048"]
    names = "qkvo"
    chunked = lambda t: t.reshape(C, 128, -1).transpose(1, 0, 2)
    k = a["L0_xattn_k"]
    padded = np.zeros((NH, 128 + D), k.dtype)
    padded[:, 128:] = k
    m, l = np.arange(128)[:, None], np.arange(128)[None, :]
    toep = np.stack([padded[:, 128 + 128 * part + l - m] for part in range(2)], axis=2)
    consts = np.zeros((128, CONSTS), np.float32)
    p = np.arange(128)
    consts[p, IDENT + p] = 1
    consts[:, BLOCK:BLOCK + 128] = p[:, None] // CH == p[None, :] // CH
    for e in range(2):
        for w in range(GH):
            consts[:, HMASK + GH * e + w] = p // HD == 2 * w + e
    ex = np.arange(E)
    consts[:, TRI:TRI + E * E] = (ex[None, :] < ex[:, None]).reshape(-1)[None, :]
    arrays = {
        "x": x,
        "xT": x.reshape(B, S, C, 128).transpose(0, 3, 2, 1),
        "ctx_rows": ctx,
        "ctx_cols": ctx.reshape(B, S, C, 128).transpose(3, 2, 0, 1),
        "WT": np.stack([chunked(a[f"L0_attn_W{n}"].T) for n in names], axis=1),
        "loraB": np.stack([a[f"L0_attn_B{n}"] for n in names], axis=1),
        "loraA": np.stack([a[f"L0_attn_A{n}"].T for n in names], axis=1),
        "bqk": np.stack([a[f"L0_attn_b{n}"].reshape(C, 128).T for n in "qk"], axis=1),
        "bvo": np.stack([a[f"L0_attn_b{n}"] for n in "vo"], axis=0),
        "skip_bias": a["fside_S2_0"].reshape(S, 1),
        "toep": toep,
        "w1T": chunked(a["L0_ffn_w1"].transpose(2, 0, 1).reshape(D, E * HID)),
        "w2T": a["L0_ffn_w2"].transpose(2, 0, 1),
        "wgT": chunked(a["L0_ffn_wg"]),
        "consts": consts,
    }
    arrays = {f"in_{n}": np.ascontiguousarray(v) for n, v in arrays.items()}
    nc = bacc.Bacc("TRN2", target_bir_lowering=False, num_devices=1)
    args = [nc.dram_tensor(f"in_{n}", arrays[f"in_{n}"].shape, mybir.dt.from_np(arrays[f"in_{n}"].dtype),
                           kind="ExternalInput").ap() for n in INS]
    out = nc.dram_tensor("out", (B, S, D), F32, kind="ExternalOutput").ap()
    program(nc, *args, out)
    r = run_bass_kernel_spmd(nc, [arrays], core_ids=[0])
    return r.results[0]["out"]
```

```python
from contextlib import ExitStack

import concourse.bass as bass
from concourse import mybir

F32 = mybir.dt.float32
F32R = mybir.dt.float32r
I32 = mybir.dt.int32
ALU = mybir.AluOpType
ACT = mybir.ActivationFunctionType
AX = mybir.AxisListType

B = 8
S = 128
D = 256
C = D // 128
HEADS, HD = 16, 16
GROUPS = 4
GH = HEADS // GROUPS
RANK = 16
LORA = 8.0 / RANK
SCALE = HD ** -0.5
NH = 16
CH = S // NH
E, TOP, HID = 8, 4, 128
EPS = 1e-5
NEWTON = 3
NEWTON_OPS = 1 + 4 * NEWTON
MATS = 4
Q, K, V, O = range(MATS)
HALVES = 2
HB = B // HALVES
CONV_BUFS = 4
TOEP_SLOTS = CONV_BUFS
EXPERT_BUFS = 4
HID_BUFS = 4
AHEAD = 2
FFN_W = C * E * HID + E * D
W_PARTS = 8
W_PART = FFN_W // W_PARTS
IDENT, BLOCK, HMASK, TRI, CONSTS = 0, 128, 256, 264, 328


def program(nc, x, xT, ctx_rows, ctx_cols, WT, loraB, loraA, bqk, bvo, skip_bias, toep, ffnT, wgT, consts, out):
    with ExitStack() as stack:
        def sb(name, shape, dt=F32):
            return stack.enter_context(nc.sbuf_tensor(name, shape, dt))

        def sem(name):
            return stack.enter_context(nc.semaphore(name))

        x_sb = sb("x_sb", [S, B, D])
        xT_sb = sb("xT_sb", [128, 2, C, S])
        ctx_r = sb("ctx_r", [S, B, D])
        ctx_c = sb("ctx_c", [128, B, C, S])
        w_sb = sb("w_sb", [128, MATS, C, D])
        kv = sb("kv", [128, CONV_BUFS, HB * C * CH * CH])
        lora_sb = kv[0:RANK].rearrange("p (t u) (v d) -> p t (u v) d", t=2, d=D)
        loraB_sb, loraA_sb = lora_sb[:, 0], lora_sb[:, 1]
        bqk_sb = sb("bqk_sb", [128, 2, C])
        bvo_sb = sb("bvo_sb", [128, 2, D])
        skip_sb = sb("skip_sb", [128, 1])
        toep_sb = sb("toep_sb", [128, TOEP_SLOTS, 2, 128])
        ffn_sb = sb("ffn_sb", [128, FFN_W // 2])
        ffn_hi = sb("ffn_hi", [128, FFN_W], F32R)
        ffn_lo = sb("ffn_lo", [128, FFN_W], F32R)
        wg_sb = sb("wg_sb", [128, C, E])
        const_sb = sb("const_sb", [128, CONSTS])
        ident = const_sb[:, IDENT:IDENT + 128]
        block_ones = const_sb[:, BLOCK:BLOCK + 128]
        head_mask = const_sb[:, HMASK:HMASK + 8].rearrange("p (e w) -> p e w", e=2)
        earlier = const_sb[:, TRI:TRI + E * E]
        qT = sb("qT", [128, 2, C, S])
        kT = sb("kT", [128, 2, C, S])
        kM = sb("kM", [128, 2, C, 2, GH, S])
        vz = sb("vz", [S, 2, C, 2, GH, 2 * HD])
        rowmax = sb("rowmax", [S, 2, GH])
        shifted = sb("shifted", [S, 2, GH * S])
        probs = sb("probs", [S, 2, GH * S])
        probsT = sb("probsT", [S, 2, GH * S])
        ones = sb("ones", [128, 2, 2 * HD])
        inv_sum = sb("inv_sum", [128, C, S])
        attnT = sb("attnT", [128, C, S])
        x1 = sb("x1", [S, B, D])
        x1_now = sb("x1_now", [S, 2, D])
        x2 = x_sb
        stats = sb("stats", [S, HB, 6])
        moments = sb("moments", [S, HB, 2])
        nw_v = sb("nw_v", [S, HB])
        nw_h = sb("nw_h", [S, HB])
        nw_a = sb("nw_a", [S, HB])
        rstd = sb("rstd", [S, HB])
        minus_half = sb("minus_half", [S, HB])
        three_halves = sb("three_halves", [S, HB])
        vT = sb("vT", [128, B, C, S])
        skip_ctx = sb("skip_ctx", [S, B, D])
        gated = direct = skip_ctx
        z = sb("z", [128, 2, HB * C * CH * CH])
        mixT = vT
        x2T = kM[:, 0].rearrange("p c e w s -> p c (e w s)")
        x2T_hi = sb("x2T_hi", [128, C, B * S], F32R)
        x2T_lo = sb("x2T_lo", [128, C, B * S], F32R)
        gateT = sb("gateT", [E, B * S])
        gate = sb("gate", [S, B, E])
        above = sb("above", [S, B, E * E])
        ties = sb("ties", [S, B, E * E])
        rank = sb("rank", [S, B, E])
        chosen = sb("chosen", [S, B, E])
        top = sb("top", [S, B])
        soft = sb("soft", [S, B, E])
        total = sb("total", [S, B])
        weight = sb("weight", [S, B, E])
        hT = probs.rearrange("p e (f s) -> p (e f) s", f=2)
        hT_hi = sb("hT_hi", [HID, HID_BUFS, 2 * S], F32R)
        hT_lo = sb("hT_lo", [HID, HID_BUFS, 2 * S], F32R)
        final = x1

        bank = [stack.enter_context(nc.psum_tensor(f"bank{i}", [128, 512], F32)) for i in range(8)]
        ps_scores, ps_turned = bank[0:2], bank[2:4]
        ps_attn, ps_qk, ps_v, ps_o = bank[4], bank[5], bank[6], bank[7]
        ps_conv, ps_turn = bank[0:4], bank[6:8]
        ps_hidden, ps_expert = bank[4:6], bank[0:4]

        ld_w, ld_lora, ld_small, ld_const = [sem("ld_wqk"), sem("ld_wvo")], sem("ld_lora"), sem("ld_small"), sem("ld_const")
        ld_x, ld_ctx, ld_wg, ld_ffn = sem("ld_x"), sem("ld_ctx"), sem("ld_wg"), sem("ld_ffn")
        ld_xT = [sem("ld_xT0"), sem("ld_xT1")]
        ld_toep = [sem(f"ld_toep{i}") for i in range(TOEP_SLOTS)]
        stored = sem("stored")
        lora_done, w_ready, cleared, xb_ready = sem("lora_done"), sem("w_ready"), sem("cleared"), sem("xb_ready")
        qk_done, v_done, qk_ready, v_ready, kM_ready = (
            sem("qk_done"), sem("v_done"), sem("qk_ready"), sem("v_ready"), sem("kM_ready"))
        scores_done, max_ready, shifted_ready, probs_ready, turned_done, probsT_ready = (
            sem("scores_done"), sem("max_ready"), sem("shifted_ready"), sem("probs_ready"), sem("turned_done"),
            sem("probsT_ready"))
        pv_done, inv_ready, attnT_ready, o_done = sem("pv_done"), sem("inv_ready"), sem("attnT_ready"), sem("o_done")
        x1_summed, x1_ready = sem("x1_summed"), sem("x1_ready")
        guessed, newton = sem("guessed"), sem("newton")
        vT_done, vT_ready, gated_ready, blocks_done, direct_ready, base_ready = (
            sem("vT_done"), sem("vT_ready"), sem("gated_ready"), sem("blocks_done"), sem("direct_ready"),
            sem("base_ready"))
        kv_ready, conv_done, z_ready, mixT_ready = sem("kv_ready"), sem("conv_done"), sem("z_ready"), sem("mixT_ready")
        mix_done, x2_summed, x2_ready = sem("mix_done"), sem("x2_summed"), sem("x2_ready")
        x2T_done, x2T_ready, gateT_done, gateT_ready, gate_done, gating, gate_exp = (
            sem("x2T_done"), sem("x2T_ready"), sem("gateT_done"), sem("gateT_ready"), sem("gate_done"),
            sem("gating"), sem("gate_exp"))
        w_hi_ready, w_lo_ready, x2T_split, h_split, skip_ready = (
            sem("w_hi_ready"), sem("w_lo_ready"), sem("x2T_split"), sem("h_split"), sem("skip_ready"))
        h_done, h_ready, expert_done, combined = sem("h_done"), sem("h_ready"), sem("expert_done"), sem("combined")
        final_ready = sem("final_ready")

        def half(n):
            return slice(HB * n, HB * n + HB)

        def w1(t, c, e):
            return t[:, c * E * HID + e * HID:c * E * HID + (e + 1) * HID]

        def w2(t, e):
            return t[:, C * E * HID + e * D:C * E * HID + (e + 1) * D]

        block = stack.enter_context(nc.Block())

        @block.sync
        def _(sp):
            sp.dma_start(w_sb[:, Q:V], WT[:, Q:V]).then_inc(ld_w[0], 16)
            sp.dma_start(xT_sb[:, 0], xT[0]).then_inc(ld_xT[0], 16)
            sp.dma_start(w_sb[:, V:], WT[:, V:]).then_inc(ld_w[1], 16)
            sp.dma_start(xT_sb[:, 1], xT[1]).then_inc(ld_xT[1], 16)
            sp.dma_start(x_sb[:], x.rearrange("b s d -> s b d")).then_inc(ld_x, 16)
            sp.dma_start(ctx_r[:], ctx_rows.rearrange("b s d -> s b d")).then_inc(ld_ctx, 16)
            sp.dma_start(ctx_c[:], ctx_cols).then_inc(ld_ctx, 16)
            for u in range(TOEP_SLOTS):
                sp.dma_start(toep_sb[:, u], toep[u]).then_inc(ld_toep[u], 16)
            sp.dma_start(wg_sb[:], wgT).then_inc(ld_wg, 16)
            sp.dma_start(ffn_sb[:], ffnT[:, 0:FFN_W // 2]).then_inc(ld_ffn, 16)
            with sp.Fori(2, B - 1, 2) as i:
                for slot in range(2):
                    sp.wait_ge(v_done, i + slot - 1)
                    sp.dma_start(xT_sb[:, slot], xT[bass.ds(i + slot, 1)].rearrange("o p c s -> (o p) c s")
                                 ).then_inc(ld_xT[slot], 16)
            sp.wait_ge(w_lo_ready, W_PARTS // 2)
            sp.dma_start(ffn_sb[:], ffnT[:, FFN_W // 2:]).then_inc(ld_ffn, 16)
            for n in range(HALVES):
                with sp.Fori(TOEP_SLOTS if n == 0 else 0, NH - TOEP_SLOTS + 1, TOEP_SLOTS) as i:
                    for u in range(TOEP_SLOTS):
                        sp.wait_ge(conv_done, NH * n + i + u - TOEP_SLOTS + 1)
                        sp.dma_start(toep_sb[:, u], toep[bass.ds(i + u, 1)].rearrange("o p k m -> (o p) k m")
                                     ).then_inc(ld_toep[u], 16)
            with sp.Fori(0, B) as b:
                sp.wait_ge(final_ready, b + 1)
                sp.dma_start(out[bass.ds(b, 1)].rearrange("o s d -> (o s) d"),
                             final[:, bass.ds(b, 1), :].rearrange("s o d -> s (o d)")).then_inc(stored, 16)
            sp.wait_ge(stored, 16 * B)

        @block.scalar
        def _(act):
            act.dma_start(loraB_sb, loraB).then_inc(ld_lora, 16)
            act.dma_start(loraA_sb, loraA).then_inc(ld_lora, 16)
            act.dma_start(const_sb[:], consts).then_inc(ld_const, 16)
            act.dma_start(bqk_sb[:], bqk).then_inc(ld_small, 16)
            act.dma_start(bvo_sb[:], bvo.partition_broadcast(128)).then_inc(ld_small, 16)
            act.dma_start(skip_sb[:], skip_bias).then_inc(ld_small, 16)

            def qk_out(b, slot):
                act.wait_ge(qk_done, b + 1)
                for c in range(C):
                    for m, buf in ((Q, qT), (K, kT)):
                        nc.scalar.activation(buf[:, slot, c], ps_qk[:, (2 * c + m) * S:(2 * c + m + 1) * S],
                                             ACT.Identity, bias=bqk_sb[:, m, c:c + 1]).then_inc(qk_ready, 1)

            def exp(G, par, first=False):
                act.wait_ge(shifted_ready, G + 1)
                if not first:
                    act.wait_ge(turned_done, G - 1)
                nc.scalar.activation(probs[:, par], shifted[:, par], ACT.Exp, scale=SCALE).then_inc(probs_ready, 1)

            def turned_out(G, par, first=False):
                act.wait_ge(turned_done, G + 1)
                if not first:
                    act.wait_ge(pv_done, G - 1)
                nc.scalar.copy(probsT[:, par], ps_turned[par][:]).then_inc(probsT_ready, 1)

            def vT_out(b):
                act.wait_ge(vT_done, b + 1)
                nc.scalar.copy(vT[:, bass.ds(b, 1)].rearrange("p o c s -> p (o c s)"), ps_v[:, D:2 * D]
                               ).then_inc(vT_ready, 1)

            def weights_hi(part, second):
                nc.scalar.copy(ffn_hi[:, bass.ds(W_PART * part, W_PART)],
                               ffn_sb[:, bass.ds(W_PART * (part - W_PARTS // 2 * second), W_PART)]).then_inc(w_hi_ready, 1)

            def step(b, slot, before=2, last=False, part=None):
                for g in range(GROUPS):
                    G = GROUPS * b + g
                    exp(G, g % 2, before == 0 and g < 2)
                    if g == 0 and not last:
                        if before:
                            act.wait_ge(scores_done, GROUPS * b)
                            act.wait_ge(kM_ready, 4 * b)
                        qk_out(b + 1, 1 - slot)
                    if g == GROUPS - 1 and before == 2:
                        vT_out(b - 2)
                    turned_out(G, g % 2, before == 0 and g < 2)
                    if g == 2 and part is not None:
                        weights_hi(part, 0)

            act.wait_ge(ld_small, 48)
            qk_out(0, 0)
            step(0, 0, before=0)
            act.wait_ge(ld_ctx, 32)
            nc.scalar.activation(skip_ctx[:].rearrange("p b d -> p (b d)"), ctx_r[:].rearrange("p b d -> p (b d)"),
                                 ACT.Copy, scale=skip_sb[:, 0:1]).then_inc(skip_ready, 1)
            step(1, 1, before=1)
            act.wait_ge(ld_ffn, 16)
            with act.Fori(2, B - 3, 2) as i:
                step(i, 0, part=i - 2)
                step(i + 1, 1, part=i - 1)
            step(B - 2, 0)
            step(B - 1, 1, last=True)
            vT_out(B - 2)
            act.wait_ge(ld_ffn, 32)
            weights_hi(W_PARTS // 2, 1)
            vT_out(B - 1)
            for part in range(W_PARTS // 2 + 1, W_PARTS):
                weights_hi(part, 1)

            def x2T_out(n):
                for q in range(2):
                    pair = 2 * n + q
                    act.wait_ge(x2T_done, pair + 1)
                    for t in (x2T, x2T_hi):
                        nc.scalar.copy(t[:].rearrange("p c (b s) -> p c b s", b=B)[:, :, 2 * pair:2 * pair + 2, :],
                                       ps_turn[q][:].rearrange("p (b c s) -> p c b s", b=2, c=C)).then_inc(x2T_ready, 1)

            def gateT_out(n):
                act.wait_ge(gateT_done, n + 1)
                nc.scalar.copy(gateT[:, n * 512:(n + 1) * 512], ps_turn[0][0:E, :]).then_inc(gateT_ready, 1)

            def gate_exponent(n):
                act.wait_ge(gating, GATING_OPS * n + GATE_SHIFTED)
                nc.scalar.activation(soft[:, half(n)], soft[:, half(n)], ACT.Exp).then_inc(gate_exp, 1)

            def relu(k, e, first=False):
                act.wait_ge(h_done, k + 1)
                if not first:
                    act.wait_ge(h_split, k - HID_BUFS + 1)
                    act.wait_ge(expert_done, k - HID_BUFS + 1)
                for t in (hT, hT_hi):
                    nc.scalar.activation(t[:, e % HID_BUFS], ps_hidden[e % 2][:, 0:2 * S], ACT.Relu).then_inc(h_ready, 1)

            x2T_out(0)
            for e in range(E):
                relu(e, e, e < HID_BUFS)
                if e == 0:
                    gateT_out(0)
                if e == 1:
                    gate_exponent(0)
                if e == 6:
                    x2T_out(1)
                if e == 7:
                    gateT_out(1)
                    gate_exponent(1)
            with act.Fori(1, B // 2) as p:
                for e in range(E):
                    relu(E * p + e, e)

        @block.gpsimd
        def _(pool):
            nc.gpsimd.memset(ones[:], 0.0).then_inc(cleared, 1)
            nc.gpsimd.memset(vz[:], 0.0).then_inc(cleared, 1)
            nc.gpsimd.memset(minus_half[:], -0.5).then_inc(cleared, 1)
            nc.gpsimd.memset(three_halves[:], 1.5).then_inc(cleared, 1)
            pool.wait_ge(cleared, 1)
            nc.gpsimd.memset(ones[:, 0, 0:HD], 1.0).then_inc(cleared, 1)
            nc.gpsimd.memset(ones[:, 1, HD:2 * HD], 1.0).then_inc(cleared, 1)

            def mask_keys(b, slot):
                for c in range(C):
                    pool.wait_ge(qk_ready, 4 * b + 2 * c + 2)
                    for e in range(2):
                        nc.gpsimd.tensor_tensor(
                            kM[:, slot, c, e], kT[:, slot, c].unsqueeze(1).to_broadcast([128, GH, S]),
                            head_mask[:, e].unsqueeze(2).to_broadcast([128, GH, S]), ALU.mult).then_inc(kM_ready, 1)

            def inverse_root(call, n, steps=range(NEWTON)):
                done = NEWTON_OPS * call
                v, hv, a, y = nw_v[:, 0:n], nw_h[:, 0:n], nw_a[:, 0:n], rstd[:, 0:n]
                if 0 in steps:
                    pool.wait_ge(guessed, call + 1)
                    nc.gpsimd.tensor_tensor(hv, v, minus_half[:, 0:n], ALU.mult).then_inc(newton, 1)
                for k in steps:
                    at = done + 1 + 4 * k
                    pool.wait_ge(newton, at)
                    nc.gpsimd.tensor_tensor(a, y, y, ALU.mult).then_inc(newton, 1)
                    pool.wait_ge(newton, at + 1)
                    nc.gpsimd.tensor_tensor(a, a, hv, ALU.mult).then_inc(newton, 1)
                    pool.wait_ge(newton, at + 2)
                    nc.gpsimd.tensor_tensor(a, a, three_halves[:, 0:n], ALU.add).then_inc(newton, 1)
                    pool.wait_ge(newton, at + 3)
                    nc.gpsimd.tensor_tensor(y, y, a, ALU.mult).then_inc(newton, 1)

            def base(b, slot):
                pool.wait_ge(direct_ready, b + 1)
                row = x1[:, bass.ds(b, 1), :].rearrange("p o d -> p (o d)")
                nc.gpsimd.tensor_tensor(row, x1_now[:, slot], direct[:, bass.ds(b, 1), :].rearrange("p o d -> p (o d)"),
                                        ALU.add).then_inc(base_ready, 1)

            def products(n, h, slot, first=False):
                k = NH * n + h
                if not first:
                    pool.wait_ge(conv_done, k - CONV_BUFS + 1)
                shape = [128, HB * C, CH, CH]
                at = lambda t: t[:, half(n), :, bass.ds(CH * h, CH)].rearrange("p b c i -> p (b c) i")
                nc.gpsimd.tensor_tensor(
                    kv[:, slot].rearrange("p (m i j) -> p m i j", i=CH, j=CH), at(vT).unsqueeze(3).to_broadcast(shape),
                    at(ctx_c).unsqueeze(2).to_broadcast(shape), ALU.mult).then_inc(kv_ready, 1)

            pool.wait_ge(ld_const, 16)
            mask_keys(0, 0)
            mask_keys(1, 1)

            def with_bias(b):
                one = x_sb[:, bass.ds(b, 1), :].rearrange("p o d -> p (o d)")
                nc.gpsimd.tensor_tensor(one, one, bvo_sb[:, 1], ALU.add).then_inc(xb_ready, 1)

            def gate_direct(b, slot):
                pool.wait_ge(x1_ready, b + 1)
                nc.gpsimd.tensor_tensor(gated[:, bass.ds(b, 1), :].rearrange("p o d -> p (o d)"), x1_now[:, slot],
                                        skip_ctx[:, bass.ds(b, 1), :].rearrange("p o d -> p (o d)"), ALU.mult
                                        ).then_inc(gated_ready, 1)

            def weights_lo(part, second):
                pool.wait_ge(w_hi_ready, part + 1)
                cut = bass.ds(W_PART * part, W_PART)
                whole = ffn_sb[:, bass.ds(W_PART * (part - W_PARTS // 2 * second), W_PART)]
                nc.gpsimd.tensor_tensor(ffn_lo[:, cut], whole, ffn_hi[:, cut].bitcast(F32), ALU.subtract
                                        ).then_inc(w_lo_ready, 1)

            pool.wait_ge(ld_x, 16)
            pool.wait_ge(ld_small, 48)
            with_bias(0)

            pool.wait_ge(cleared, 6)

            def step(b, slot, before=2, last=False, part=None):
                if not last:
                    pool.wait_ge(scores_done, GROUPS * b)
                    mask_keys(b + 1, 1 - slot)
                with_bias(b)
                if before == 2:
                    gate_direct(b - 2, slot)
                inverse_root(b - 1, 1)
                if part is not None:
                    weights_lo(part, 0)
                if before == 2:
                    base(b - 2, slot)

            step(1, 1, before=1)
            pool.wait_ge(skip_ready, 1)
            with pool.Fori(2, B - 3, 2) as i:
                step(i, 0, part=i - 2)
                step(i + 1, 1, part=i - 1)
            step(B - 2, 0)
            pool.wait_ge(ld_ctx, 32)
            pool.wait_ge(vT_ready, HB)
            products(0, 0, 0, True)
            products(0, 1, 1, True)
            step(B - 1, 1, last=True)
            products(0, 2, 2, True)
            products(0, 3, 3, True)
            gate_direct(B - 2, 0)
            inverse_root(B - 1, 1)
            products(0, 4, 0)
            gate_direct(B - 1, 1)
            products(0, 5, 1)
            base(B - 2, 0)
            products(0, 6, 2)
            base(B - 1, 1)
            products(0, 7, 3)
            with pool.Fori(8, NH - 3, CONV_BUFS) as i:
                for u in range(CONV_BUFS):
                    products(0, i + u, u)
            pool.wait_ge(vT_ready, B)
            with pool.Fori(0, NH - 7, CONV_BUFS) as i:
                for u in range(CONV_BUFS):
                    products(1, i + u, u)
            inverse_root(B, HB)
            for u in range(CONV_BUFS):
                products(1, NH - CONV_BUFS + u, u)
            for part in range(W_PARTS // 2, W_PARTS):
                weights_lo(part, 1)

            def split_x2T(pair):
                pool.wait_ge(x2T_ready, 2 * pair + 2)
                at = lambda t: t[:, :, 2 * S * pair:2 * S * (pair + 1)]
                nc.gpsimd.tensor_tensor(at(x2T_lo), at(x2T), at(x2T_hi).bitcast(F32), ALU.subtract).then_inc(x2T_split, 1)

            def split_hidden(k, e, first=False):
                pool.wait_ge(h_ready, 2 * k + 2)
                if not first:
                    pool.wait_ge(expert_done, k - HID_BUFS + 1)
                u = e % HID_BUFS
                nc.gpsimd.tensor_tensor(hT_lo[:, u], hT[:, u], hT_hi[:, u].bitcast(F32), ALU.subtract).then_inc(h_split, 1)

            split_x2T(0)
            split_x2T(1)
            for e in range(E):
                split_hidden(e, e, e < HID_BUFS)
                if e == 1:
                    inverse_root(B + 1, HB)
                if e == 6:
                    split_x2T(2)
                    split_x2T(3)
            with pool.Fori(1, B // 2) as p:
                for e in range(E):
                    split_hidden(E * p + e, e)
                    if 3 <= e < 3 + NEWTON:
                        inverse_root(B + 1 + p, 2, (e - 3,))
            inverse_root(B + 1 + B // 2, 2)

        @block.vector
        def _(dve):
            def row(t, b):
                return t[:, bass.ds(b, 1), :].rearrange("p o d -> p (o d)")

            def statistics(rows):
                n = len(rows)
                dve.drain()
                for u, r in enumerate(rows):
                    nc.vector.bn_stats(stats[:, u], r)
                dve.drain()
                for u in range(n):
                    nc.vector.bn_aggr(moments[:, u], stats[:, u])
                dve.drain()
                v, y = nw_v[:, 0:n], rstd[:, 0:n]
                nc.vector.tensor_scalar(v, moments[:, 0:n, 1], EPS, None, ALU.add)
                dve.drain()
                nc.vector.tensor_scalar(y.bitcast(I32), v.bitcast(I32), -0.5, float(0x5F3759DF), ALU.mult,
                                        ALU.add).then_inc(guessed, 1)

            def layernorm(call, rows, outs, ready):
                dve.wait_ge(newton, NEWTON_OPS * (call + 1))
                for u, (r, o) in enumerate(zip(rows, outs)):
                    nc.vector.tensor_scalar(o, r, moments[:, u, 0:1], rstd[:, u:u + 1], ALU.subtract,
                                            ALU.mult).then_inc(ready, 1)

            for m in range(MATS):
                dve.wait_ge(ld_w[m // 2], 16)
                dve.wait_ge(lora_done, m + 1)
                nc.vector.scalar_tensor_tensor(
                    out=w_sb[:, m].rearrange("p c d -> p (c d)"), in0=bank[m][:], scalar=LORA,
                    in1=w_sb[:, m].rearrange("p c d -> p (c d)"), op0=ALU.mult, op1=ALU.add).then_inc(w_ready, 1)

            def v_out(b, slot):
                dve.wait_ge(v_done, b + 1)
                for e in range(2):
                    cut = lambda t: t.rearrange("p (c w e d) -> p c w e d", c=C, w=GH, e=2)[:, :, :, e, :]
                    nc.vector.tensor_tensor(vz[:, slot, :, e, :, HD * e:HD * (e + 1)], cut(ps_v[:, 0:D]),
                                            cut(bvo_sb[:, 0]), ALU.add).then_inc(v_ready, 1)

            def shift(G, par, first=False):
                dve.wait_ge(scores_done, G + 1)
                scores = ps_scores[par][:].rearrange("p (h k) -> p h k", h=GH)
                nc.vector.tensor_reduce(rowmax[:, par], scores, AX.X, ALU.max).then_inc(max_ready, 1)
                dve.wait_ge(max_ready, G + 1)
                if not first:
                    dve.wait_ge(probs_ready, G - 1)
                nc.vector.tensor_tensor(shifted[:, par].rearrange("p (h k) -> p h k", h=GH), scores,
                                        rowmax[:, par].unsqueeze(2).to_broadcast([S, GH, S]),
                                        ALU.subtract).then_inc(shifted_ready, 1)

            def normalise(b):
                dve.wait_ge(pv_done, GROUPS * b + GROUPS)
                nc.vector.reciprocal(inv_sum[:].rearrange("p c s -> p (c s)"), ps_attn[:, D:2 * D]).then_inc(inv_ready, 1)
                dve.wait_ge(inv_ready, b + 1)
                nc.vector.tensor_tensor(attnT[:].rearrange("p c s -> p (c s)"), ps_attn[:, 0:D],
                                        inv_sum[:].rearrange("p c s -> p (c s)"), ALU.mult).then_inc(attnT_ready, 1)

            def residual(b):
                dve.wait_ge(o_done, b + 1)
                nc.vector.tensor_tensor(row(x1, b), ps_o[:, 0:D], row(x_sb, b), ALU.add).then_inc(x1_summed, 1)
                statistics([row(x1, b)])

            def direct_out(b):
                dve.wait_ge(blocks_done, b + 1)
                nc.vector.tensor_tensor(row(direct, b), ps_o[:, D:2 * D], row(ctx_r, b), ALU.mult
                                        ).then_inc(direct_ready, 1)

            def step(b, slot, before=2, last=False):
                G = GROUPS * b
                shift(G, 0, before == 0)
                shift(G + 1, 1, before == 0)
                if before:
                    normalise(b - 1)
                shift(G + 2, 0)
                if not last:
                    v_out(b + 1, 1 - slot)
                if before == 2:
                    layernorm(b - 2, [row(x1, b - 2)], [x1_now[:, slot]], x1_ready)
                shift(G + 3, 1)
                if before:
                    dve.wait_ge(xb_ready, b)
                    residual(b - 1)
                if before == 2:
                    direct_out(b - 2)

            dve.wait_ge(ld_small, 48)
            dve.wait_ge(cleared, 6)
            v_out(0, 0)
            step(0, 0, before=0)
            step(1, 1, before=1)
            dve.wait_ge(ld_ctx, 32)
            with dve.Fori(2, B - 3, 2) as i:
                step(i, 0)
                step(i + 1, 1)
            step(B - 2, 0)
            step(B - 1, 1, last=True)

            def query(n, h, k, par, first=False):
                dve.wait_ge(conv_done, k + 1)
                if not first:
                    dve.wait_ge(mixT_ready, k - 1)
                nc.vector.tensor_tensor(
                    z[:, par % 2].rearrange("p (m i j) -> p m i j", i=CH, j=CH),
                    ps_conv[par][:].rearrange("p (m i j) -> p m i j", i=CH, j=CH),
                    ctx_c[:, half(n), :, bass.ds(CH * h, CH)].rearrange("p b c i -> p (b c) i").unsqueeze(3)
                    .to_broadcast([128, HB * C, CH, CH]), ALU.mult).then_inc(z_ready, 1)

            def gather(n, h, k, par):
                dve.wait_ge(z_ready, k + 1)
                nc.vector.tensor_reduce(
                    mixT[:, half(n), :, bass.ds(CH * h, CH)].rearrange("p b c i -> p (b c) i"),
                    z[:, par % 2].rearrange("p (m i j) -> p m j i", i=CH, j=CH), AX.X, ALU.add).then_inc(mixT_ready, 1)

            def two_heads(n, h, u):
                k = NH * n + h
                first = isinstance(k, int) and k == 0
                query(n, h, k, u, first)
                query(n, h + 1, k + 1, u + 1, first)
                gather(n, h, k, u)
                gather(n, h + 1, k + 1, u + 1)

            normalise(B - 1)
            layernorm(B - 2, [x1[:, B - 2]], [x1_now[:, 0]], x1_ready)
            dve.wait_ge(xb_ready, B)
            residual(B - 1)
            direct_out(B - 2)
            two_heads(0, 0, 0)
            layernorm(B - 1, [x1[:, B - 1]], [x1_now[:, 1]], x1_ready)
            two_heads(0, 2, 2)
            direct_out(B - 1)
            with dve.Fori(CONV_BUFS, NH - 3, CONV_BUFS) as i:
                two_heads(0, i, 0)
                two_heads(0, i + 2, 2)

            def x2_sum(n):
                for b in range(HB * n, HB * n + HB):
                    if b % 2 == 0:
                        dve.wait_ge(mix_done, b // 2 + 1)
                    dve.wait_ge(base_ready, b + 1)
                    nc.vector.tensor_tensor(x2[:, b], ps_turn[b // 2 % 2][:, (b % 2) * D:(b % 2 + 1) * D], x1[:, b],
                                            ALU.add).then_inc(x2_summed, 1)
                statistics([x2[:, b] for b in range(HB * n, HB * n + HB)])

            def x2_norm(n):
                rows = [x2[:, b] for b in range(HB * n, HB * n + HB)]
                layernorm(B + n, rows, rows, x2_ready)

            two_heads(1, 0, 0)
            two_heads(1, 2, 2)
            x2_sum(0)
            with dve.Fori(CONV_BUFS, NH - 7, CONV_BUFS) as i:
                two_heads(1, i, 0)
                two_heads(1, i + 2, 2)
            x2_norm(0)
            two_heads(1, NH - 4, 0)
            two_heads(1, NH - 2, 2)
            x2_sum(1)

            def gates(n):
                count = [GATING_OPS * n]

                def link(ins):
                    count[0] += 1
                    ins.then_inc(gating, 1)
                    dve.wait_ge(gating, count[0])

                h = half(n)
                full, pair = [S, HB, E], [S, HB, E, E]
                four = lambda t: t[:, h].rearrange("p b (e f) -> p b e f", e=E)
                dve.wait_ge(gate_done, n + 1)
                link(nc.vector.tensor_copy(gate[:, h].rearrange("p b e -> p (b e)"), (ps_expert[3], ps_turn[1])[n][:, 0:HB * E]))
                link(nc.vector.tensor_reduce(top[:, h], gate[:, h], AX.X, ALU.max))
                link(nc.vector.tensor_tensor(soft[:, h], gate[:, h], top[:, h].unsqueeze(2).to_broadcast(full), ALU.subtract))
                theirs = gate[:, h].unsqueeze(2).to_broadcast(pair)
                own = gate[:, h].unsqueeze(3).to_broadcast(pair)
                link(nc.vector.tensor_tensor(four(above), theirs, own, ALU.is_gt))
                link(nc.vector.tensor_tensor(four(ties), theirs, own, ALU.is_equal))
                link(nc.vector.tensor_tensor(ties[:, h], ties[:, h], earlier.unsqueeze(1).to_broadcast([S, HB, E * E]),
                                             ALU.mult))
                link(nc.vector.tensor_tensor(above[:, h], above[:, h], ties[:, h], ALU.add))
                link(nc.vector.tensor_reduce(rank[:, h], four(above), AX.X, ALU.add))
                link(nc.vector.tensor_scalar(chosen[:, h], rank[:, h], float(TOP), None, ALU.is_lt))
                dve.wait_ge(gate_exp, n + 1)
                link(nc.vector.tensor_tensor(soft[:, h], soft[:, h], chosen[:, h], ALU.mult))
                link(nc.vector.tensor_reduce(total[:, h], soft[:, h], AX.X, ALU.add))
                link(nc.vector.reciprocal(total[:, h], total[:, h]))
                link(nc.vector.tensor_tensor(soft[:, h], soft[:, h], total[:, h].unsqueeze(2).to_broadcast(full), ALU.mult))
                link(nc.vector.tensor_scalar(weight[:, h], soft[:, h], 1.0, None, ALU.add))
                link(nc.vector.tensor_tensor(weight[:, h], weight[:, h], soft[:, h], ALU.subtract))
                link(nc.vector.tensor_tensor(weight[:, h], weight[:, h], chosen[:, h], ALU.mult))

            def combine(p, e, first=False):
                k = E * p + e
                dve.wait_ge(expert_done, k + 1)
                for u in range(2):
                    if not first:
                        dve.wait_ge(combined, 2 * k + u - 1)
                    nc.vector.scalar_tensor_tensor(
                        out=row(x2, 2 * p + u), in0=ps_expert[e % EXPERT_BUFS][:, u * D:(u + 1) * D],
                        scalar=row(weight, 2 * p + u)[:, e:e + 1], in1=row(x2, 2 * p + u),
                        op0=ALU.mult, op1=ALU.add).then_inc(combined, 1)

            def finish(p):
                layernorm(B + 2 + p, [row(x2, 2 * p + u) for u in range(2)],
                          [row(final, 2 * p + u) for u in range(2)], final_ready)

            gates(0)
            for e in range(E):
                combine(0, e, e == 0)
                if e == 1:
                    x2_norm(1)
                if e == 6:
                    gates(1)
            statistics([x2[:, 0], x2[:, 1]])
            with dve.Fori(1, B // 2) as p:
                for e in range(E):
                    combine(p, e)
                    if e == 5:
                        finish(p - 1)
                statistics([row(x2, 2 * p), row(x2, 2 * p + 1)])
            finish(B // 2 - 1)

        @block.tensor
        def _(pe):
            mm = nc.tensor.matmul
            turn_block = nc.tensor.transpose
            pe.wait_ge(ld_lora, 32)

            def lora(m):
                for c in range(C):
                    last = mm(bank[m][:, c * D:(c + 1) * D], loraB_sb[:, m, c * 128:(c + 1) * 128], loraA_sb[:, m],
                              start=True, stop=True)
                last.then_inc(lora_done, 1)

            def project_qk(b, slot, first=False):
                pe.wait_ge(ld_xT[slot], 8 * (b - slot) + 16)
                if not first:
                    pe.wait_ge(qk_ready, 4 * b)
                for c in range(C):
                    for m in (Q, K):
                        at = 2 * c + m
                        for d in range(C):
                            last = mm(ps_qk[:, at * S:(at + 1) * S], w_sb[:, m, d, c * 128:(c + 1) * 128],
                                      xT_sb[:, slot, d], start=(d == 0), stop=(d == C - 1))
                last.then_inc(qk_done, 1)

            def project_v(b, slot, first=False):
                if not first:
                    pe.wait_ge(v_ready, 2 * b)
                for d in range(C):
                    last = mm(ps_v[:, 0:D], xT_sb[:, slot, d], w_sb[:, V, d], start=(d == 0), stop=(d == C - 1))
                last.then_inc(v_done, 1)

            def scores(b, g, slot, first=False):
                c, e = g // 2, g % 2
                if e == 0:
                    pe.wait_ge(qk_ready, 4 * b + 2 * c + 1)
                pe.wait_ge(kM_ready, 4 * b + 2 * c + e + 1)
                if not first:
                    pe.wait_ge(shifted_ready, GROUPS * b + g - 1)
                mm(ps_scores[e][:], qT[:, slot, c], kM[:, slot, c, e].rearrange("p w s -> p (w s)"), start=True,
                   stop=True).then_inc(scores_done, 1)

            def turn(G, par, first=False):
                pe.wait_ge(probs_ready, G + 1)
                if not first:
                    pe.wait_ge(probsT_ready, G - 1)
                for n in range(GH):
                    last = turn_block(ps_turned[par][:, n * S:(n + 1) * S], probs[:, par, n * S:(n + 1) * S], ident)
                last.then_inc(turned_done, 1)

            def weigh(b, g, slot, first=False):
                c, e = g // 2, g % 2
                G = GROUPS * b + g
                pe.wait_ge(probsT_ready, G + 1)
                if g == 0:
                    pe.wait_ge(v_ready, 2 * b + 2)
                    if not first:
                        pe.wait_ge(attnT_ready, b)
                for part in range(2):
                    for w in range(GH):
                        rows = slice(32 * w, 32 * w + 32)
                        lhsT = vz[:, slot, c, e, w] if part == 0 else ones[:, e]
                        last = mm(ps_attn[rows, part * D + c * S:part * D + (c + 1) * S], lhsT,
                                  probsT[:, e, w * S:(w + 1) * S], start=(g == 0 and part == 0),
                                  stop=(g == GROUPS - 1 and part == 1), skip_group_check=True)
                last.then_inc(pv_done, 1)

            def project_o(b):
                pe.wait_ge(attnT_ready, b + 1)
                for c in range(C):
                    last = mm(ps_o[:, 0:D], attnT[:, c], w_sb[:, O, c], start=(c == 0), stop=(c == C - 1))
                last.then_inc(o_done, 1)

            def turn_x1(b, slot, v_before):
                pe.wait_ge(v_ready, 2 * v_before)
                pe.wait_ge(x1_ready, b + 1)
                for c in range(C):
                    last = turn_block(ps_v[:, D + c * 128:D + (c + 1) * 128],
                                      x1_now[:, slot, c * 128:(c + 1) * 128], ident)
                last.then_inc(vT_done, 1)

            def sum_channels(b, x1_before):
                pe.wait_ge(gated_ready, b + 1)
                pe.wait_ge(x1_summed, x1_before)
                mm(ps_o[:, D:2 * D], block_ones, gated[:, bass.ds(b, 1), :].rearrange("p o d -> p (o d)"),
                   start=True, stop=True).then_inc(blocks_done, 1)

            def step(b, slot, before=2, last=False):
                for g in range(GROUPS):
                    if g < GROUPS - 1:
                        scores(b, g + 1, slot, before == 0 and g == 0)
                    elif not last:
                        scores(b + 1, 0, 1 - slot)
                    if g == 0 and not last:
                        project_qk(b + 1, 1 - slot)
                    if g == 1 and not last:
                        project_v(b + 1, 1 - slot)
                    if g == 2 and before:
                        project_o(b - 1)
                    if g == GROUPS - 1 and before == 2:
                        turn_x1(b - 2, slot, B if last else b + 2)
                    turn(GROUPS * b + g, g % 2, before == 0 and g < 2)
                    if g > 0:
                        weigh(b, g - 1, slot, before == 0)
                    elif before:
                        weigh(b - 1, GROUPS - 1, 1 - slot)
                if before == 2:
                    sum_channels(b - 2, b)
                    pe.wait_ge(vT_ready, b - 1)

            for m in range(MATS):
                lora(m)
            pe.wait_ge(w_ready, K + 1)
            project_qk(0, 0, True)
            pe.wait_ge(w_ready, MATS)
            project_v(0, 0, True)
            pe.wait_ge(ld_const, 16)
            pe.wait_ge(cleared, 6)
            scores(0, 0, 0, True)
            step(0, 0, before=0)
            step(1, 1, before=1)
            with pe.Fori(2, B - 3, 2) as i:
                step(i, 0)
                step(i + 1, 1)
            step(B - 2, 0)
            step(B - 1, 1, last=True)
            weigh(B - 1, GROUPS - 1, 1)

            def convolve(k, slot, first=False):
                pe.wait_ge(ld_toep[slot], 4 * (k - slot) + 16)
                pe.wait_ge(kv_ready, k + 1)
                if not first:
                    pe.wait_ge(z_ready, k - CONV_BUFS + 1)
                near, far = toep_sb[:, slot, 0], toep_sb[:, slot, 1]
                chunk = lambda t, c: t.rearrange("p (b c n) -> p b c n", b=HB, c=C)[:, :, c]
                mm(ps_conv[slot][:], near, kv[:, slot], start=True, stop=False)
                mm(chunk(ps_conv[slot][:], 1), far, chunk(kv[:, slot], 0), start=False, stop=True).then_inc(conv_done, 1)

            convolve(0, 0, True)
            project_o(B - 1)
            turn_x1(B - 2, 0, B)
            convolve(1, 1, True)
            sum_channels(B - 2, B)
            convolve(2, 2, True)
            convolve(3, 3, True)
            pe.wait_ge(vT_ready, B - 1)
            turn_x1(B - 1, 1, B)
            pe.wait_ge(direct_ready, B - 1)
            sum_channels(B - 1, B)
            with pe.Fori(CONV_BUFS, NH - 3, CONV_BUFS) as i:
                for u in range(CONV_BUFS):
                    convolve(i + u, u)

            def turn_mix(n):
                for b in range(HB * n, HB * n + HB):
                    for c in range(C):
                        at = (b % 2) * D + c * 128
                        last = turn_block(ps_turn[b // 2 % 2][:, at:at + 128], mixT[:, b, c], ident)
                    if b % 2:
                        last.then_inc(mix_done, 1)

            def turn_x2(n):
                for b in range(HB * n, HB * n + HB):
                    pe.wait_ge(x2_ready, b + 1)
                    for c in range(C):
                        at = (b % 2) * D + c * 128
                        last = turn_block(ps_turn[b // 2 % 2][:, at:at + 128], x2[:, b, c * 128:(c + 1) * 128], ident)
                    if b % 2:
                        last.then_inc(x2T_done, 1)

            def gate_columns(n):
                pe.wait_ge(x2T_ready, 4 * n + 4)
                for c in range(C):
                    last = mm(ps_turn[0][0:E, :], wg_sb[:, c], x2T[:, c, n * 512:(n + 1) * 512], start=(c == 0),
                              stop=(c == C - 1))
                last.then_inc(gateT_done, 1)

            def gate_rows(n):
                pe.wait_ge(gateT_ready, n + 1)
                for q in range(HB):
                    b = HB * n + q
                    last = turn_block((ps_expert[3], ps_turn[1])[n][:, q * E:(q + 1) * E], gateT[:, b * S:(b + 1) * S], ident[0:E, 0:E])
                last.then_inc(gate_done, 1)

            for u in range(CONV_BUFS):
                convolve(NH + u, u)
            pe.wait_ge(mixT_ready, NH)
            pe.wait_ge(vT_ready, B)
            pe.wait_ge(direct_ready, B)
            turn_mix(0)
            with pe.Fori(CONV_BUFS, NH - 7, CONV_BUFS) as i:
                for u in range(CONV_BUFS):
                    convolve(NH + i + u, u)
            for u in range(CONV_BUFS):
                convolve(2 * NH - CONV_BUFS + u, u)
                if u == 1:
                    turn_x2(0)

            def passes(out, hi, lo, rhs_hi, rhs_lo, start, stop):
                mm(out, lo, rhs_hi, start=start, stop=False)
                mm(out, hi, rhs_lo, start=False, stop=False)
                return mm(out, hi, rhs_hi, start=False, stop=stop)

            def hidden(p, e, first=False):
                k = E * p + e
                if e == 0:
                    pe.wait_ge(x2T_split, p + 1)
                if not first:
                    pe.wait_ge(h_ready, 2 * k - 2)
                for c in range(C):
                    at = lambda t: t[:, c, bass.ds(2 * S * p, 2 * S)]
                    last = passes(ps_hidden[e % 2][:, 0:2 * S], w1(ffn_hi, c, e), w1(ffn_lo, c, e), at(x2T_hi), at(x2T_lo),
                                  c == 0, c == C - 1)
                last.then_inc(h_done, 1)

            def expert(p, e, first=False):
                k = E * p + e
                pe.wait_ge(h_split, k + 1)
                if not first:
                    pe.wait_ge(combined, 2 * (k - EXPERT_BUFS) + 2)
                for u in range(2):
                    at = lambda t: t[:, e % HID_BUFS, u * S:(u + 1) * S]
                    last = passes(ps_expert[e % EXPERT_BUFS][:, u * D:(u + 1) * D], at(hT_hi), at(hT_lo), w2(ffn_hi, e),
                                  w2(ffn_lo, e), True, True)
                last.then_inc(expert_done, 1)

            def pair_of_entries(p, first=False, last=False):
                for e in range(E):
                    if e + AHEAD < E:
                        hidden(p, e + AHEAD)
                    elif not last:
                        hidden(p + 1, e + AHEAD - E)
                    if first and e == 3:
                        pe.wait_ge(gating, 1)
                    expert(p, e, first and e < EXPERT_BUFS)
                    if first and e == 4:
                        turn_x2(1)
                    if first and e == 5:
                        gate_columns(1)
                    if first and e == 6:
                        gate_rows(1)

            pe.wait_ge(ld_wg, 16)
            pe.wait_ge(w_lo_ready, B)
            hidden(0, 0, True)
            hidden(0, 1, True)
            gate_columns(0)
            pe.wait_ge(z_ready, 2 * NH)
            gate_rows(0)
            pe.wait_ge(mixT_ready, 2 * NH)
            turn_mix(1)
            pair_of_entries(0, first=True)
            with pe.Fori(1, B // 2 - 1) as p:
                pair_of_entries(p)
            pair_of_entries(B // 2 - 1, last=True)


GATE_SHIFTED = 3
GATING_OPS = 16


INS = ["x", "xT", "ctx_rows", "ctx_cols", "WT", "loraB", "loraA", "bqk", "bvo", "skip_bias", "toep", "ffnT", "wgT",
       "consts"]


def kernel(**inputs):
    import numpy as np
    import concourse.bacc as bacc
    from concourse.bass_utils import run_bass_kernel_spmd

    a = {k: np.asarray(v) for k, v in inputs.items()}
    x, ctx = a["x"], a["ctx_2048"]
    names = "qkvo"
    chunked = lambda t: t.reshape(C, 128, -1).transpose(1, 0, 2)
    k = a["L0_xattn_k"]
    padded = np.zeros((NH, 128 + D), k.dtype)
    padded[:, 128:] = k
    m, l = np.arange(128)[:, None], np.arange(128)[None, :]
    toep = np.stack([padded[:, 128 + 128 * part + l - m] for part in range(2)], axis=2)
    consts = np.zeros((128, CONSTS), np.float32)
    p = np.arange(128)
    consts[p, IDENT + p] = 1
    consts[:, BLOCK:BLOCK + 128] = p[:, None] // CH == p[None, :] // CH
    for e in range(2):
        for w in range(GH):
            consts[:, HMASK + GH * e + w] = p // HD == 2 * w + e
    ex = np.arange(E)
    consts[:, TRI:TRI + E * E] = (ex[None, :] < ex[:, None]).reshape(-1)[None, :]
    arrays = {
        "x": x,
        "xT": x.reshape(B, S, C, 128).transpose(0, 3, 2, 1),
        "ctx_rows": ctx,
        "ctx_cols": ctx.reshape(B, S, C, 128).transpose(3, 0, 2, 1),
        "WT": np.stack([chunked(a[f"L0_attn_W{n}"].T) for n in names], axis=1),
        "loraB": np.stack([a[f"L0_attn_B{n}"] for n in names], axis=1),
        "loraA": np.stack([a[f"L0_attn_A{n}"].T for n in names], axis=1),
        "bqk": np.stack([a[f"L0_attn_b{n}"].reshape(C, 128).T for n in "qk"], axis=1),
        "bvo": np.stack([a[f"L0_attn_b{n}"] for n in "vo"], axis=0),
        "skip_bias": a["fside_S2_0"].reshape(S, 1),
        "toep": toep,
        "ffnT": np.concatenate([chunked(a["L0_ffn_w1"].transpose(2, 0, 1).reshape(D, E * HID)).reshape(128, -1),
                                a["L0_ffn_w2"].transpose(2, 0, 1).reshape(HID, -1)], axis=1),
        "wgT": chunked(a["L0_ffn_wg"]),
        "consts": consts,
    }
    arrays = {f"in_{n}": np.ascontiguousarray(v) for n, v in arrays.items()}
    nc = bacc.Bacc("TRN2", target_bir_lowering=False, num_devices=1)
    args = [nc.dram_tensor(f"in_{n}", arrays[f"in_{n}"].shape, mybir.dt.from_np(arrays[f"in_{n}"].dtype),
                           kind="ExternalInput").ap() for n in INS]
    out = nc.dram_tensor("out", (B, S, D), F32, kind="ExternalOutput").ap()
    program(nc, *args, out)
    r = run_bass_kernel_spmd(nc, [arrays], core_ids=[0])
    return r.results[0]["out"]
```

```python
from contextlib import ExitStack

import concourse.bass as bass
from concourse import mybir

F32 = mybir.dt.float32
F32R = mybir.dt.float32r
I32 = mybir.dt.int32
ALU = mybir.AluOpType
ACT = mybir.ActivationFunctionType
AX = mybir.AxisListType

B = 8
S = 128
D = 256
C = D // 128
HEADS, HD = 16, 16
GROUPS = 4
GH = HEADS // GROUPS
RANK = 16
LORA = 8.0 / RANK
SCALE = HD ** -0.5
NH = 16
CH = S // NH
E, TOP, HID = 8, 4, 128
EPS = 1e-5
NEWTON = 3
NEWTON_OPS = 1 + 4 * NEWTON
MATS = 4
Q, K, V, O = range(MATS)
HALVES = 2
HB = B // HALVES
CONV_BUFS = 4
TOEP_SLOTS = CONV_BUFS
EXPERT_BUFS = 4
HID_BUFS = 4
ROOT_AT = 4, 6, 7
WARM = 13
AHEAD = 2
FFN_W = C * E * HID + E * D
W_PARTS = 8
W_PART = FFN_W // W_PARTS
IDENT, BLOCK, HMASK, TRI, CONSTS = 0, 128, 256, 264, 328


def program(nc, x, xT, ctx_rows, ctx_cols, WT, loraB, loraA, bqk, bvo, skip_bias, toep, ffnT, wgT, consts, out):
    with ExitStack() as stack:
        def sb(name, shape, dt=F32):
            return stack.enter_context(nc.sbuf_tensor(name, shape, dt))

        def sem(name):
            return stack.enter_context(nc.semaphore(name))

        x_sb = sb("x_sb", [S, B, D])
        xT_sb = sb("xT_sb", [128, 2, C, S])
        ctx_r = sb("ctx_r", [S, B, D])
        ctx_c = sb("ctx_c", [128, B, C, S])
        w_sb = sb("w_sb", [128, MATS, C, D])
        kv = sb("kv", [128, CONV_BUFS, HB * C * CH * CH])
        lora_sb = kv[0:RANK].rearrange("p (t u) (v d) -> p t (u v) d", t=2, d=D)
        loraB_sb, loraA_sb = lora_sb[:, 0], lora_sb[:, 1]
        bqk_sb = sb("bqk_sb", [128, 2, C])
        bvo_sb = sb("bvo_sb", [128, 2, D])
        skip_sb = sb("skip_sb", [128, 1])
        toep_sb = sb("toep_sb", [128, TOEP_SLOTS, 2, 128])
        ffn_sb = sb("ffn_sb", [128, FFN_W // 2])
        ffn_hi = sb("ffn_hi", [128, FFN_W], F32R)
        ffn_lo = sb("ffn_lo", [128, FFN_W], F32R)
        wg_sb = sb("wg_sb", [128, C, E])
        const_sb = sb("const_sb", [128, CONSTS])
        ident = const_sb[:, IDENT:IDENT + 128]
        block_ones = const_sb[:, BLOCK:BLOCK + 128]
        head_mask = const_sb[:, HMASK:HMASK + 8].rearrange("p (e w) -> p e w", e=2)
        earlier = const_sb[:, TRI:TRI + E * E]
        warm = sb("warm", [128, S])
        warmed = sb("warmed", [128, 1])
        qT = sb("qT", [128, 2, C, S])
        kT = sb("kT", [128, 2, C, S])
        kM = sb("kM", [128, 2, C, 2, GH, S])
        vz = sb("vz", [S, 2, C, 2, GH, 2 * HD])
        rowmax = sb("rowmax", [S, 2, GH])
        bound = sb("bound", [S, 2, GH])
        prob_sum = sb("prob_sum", [S, 2, GH])
        inv_sum = sb("inv_sum", [S, 2, GH])
        probs = sb("probs", [S, 2, GH * S])
        probsT = sb("probsT", [S, 2, GH * S])
        attnT = sb("attnT", [128, C, S])
        x1 = sb("x1", [S, B, D])
        x1_now = sb("x1_now", [S, 2, D])
        x2 = x_sb
        stats = sb("stats", [S, HB, 6])
        moments = sb("moments", [S, HB, 2])
        nw_v = sb("nw_v", [S, HB])
        nw_h = sb("nw_h", [S, HB])
        nw_a = sb("nw_a", [S, HB])
        rstd = sb("rstd", [S, HB])
        minus_half = sb("minus_half", [S, HB])
        three_halves = sb("three_halves", [S, HB])
        minus_one = sb("minus_one", [S, HB])
        offset = sb("offset", [S, HB])
        vT = sb("vT", [128, B, C, S])
        skip_ctx = sb("skip_ctx", [S, B, D])
        gated = direct = skip_ctx
        z = sb("z", [128, 2, HB * C * CH * CH])
        mixT = vT
        x2T = kM[:, 0].rearrange("p c e w s -> p c (e w s)")
        x2T_hi = sb("x2T_hi", [128, C, B * S], F32R)
        x2T_lo = sb("x2T_lo", [128, C, B * S], F32R)
        gate = sb("gate", [S, B, E])
        above = sb("above", [S, B, E * E])
        ties = sb("ties", [S, B, E * E])
        rank = sb("rank", [S, B, E])
        chosen = sb("chosen", [S, B, E])
        top = sb("top", [S, B])
        soft = sb("soft", [S, B, E])
        total = sb("total", [S, B])
        weight = sb("weight", [S, B, E])
        hT = probs.rearrange("p e (f s) -> p (e f) s", f=2)
        hT_hi = sb("hT_hi", [HID, HID_BUFS, 2 * S], F32R)
        hT_lo = sb("hT_lo", [HID, HID_BUFS, 2 * S], F32R)
        final = x1

        bank = [stack.enter_context(nc.psum_tensor(f"bank{i}", [128, 512], F32)) for i in range(8)]
        ps_scores, ps_turned = bank[0:2], bank[2:4]
        ps_attn, ps_qk, ps_v, ps_o = bank[4], bank[5], bank[6], bank[7]
        ps_lora = bank[4:8]
        ps_conv, ps_turn = [bank[5], *bank[0:3]], bank[6:8]
        ps_hidden, ps_expert = bank[3:5], [*bank[0:3], bank[5]]
        ps_gates = ps_expert[3], ps_turn[0]

        ld_w, ld_lora, ld_small, ld_const = [sem("ld_wqk"), sem("ld_wvo")], sem("ld_lora"), sem("ld_small"), sem("ld_const")
        ld_x, ld_ctx_rows, ld_ctx_cols = sem("ld_x"), sem("ld_ctx_rows"), sem("ld_ctx_cols")
        ld_wg, ld_ffn = sem("ld_wg"), sem("ld_ffn")
        ld_xT = [sem("ld_xT0"), sem("ld_xT1")]
        ld_toep = [sem(f"ld_toep{i}") for i in range(TOEP_SLOTS)]
        stored = sem("stored")
        lora_done, w_ready, cleared, xb_ready = sem("lora_done"), sem("w_ready"), sem("cleared"), sem("xb_ready")
        warm_ready = sem("warm_ready")
        qk_done, v_done, qk_ready, v_ready, kM_ready = (
            sem("qk_done"), sem("v_done"), sem("qk_ready"), sem("v_ready"), sem("kM_ready"))
        scores_done, max_ready, bound_ready, probs_ready, inv_ready, scaled_ready, turned_done, probsT_ready = (
            sem("scores_done"), sem("max_ready"), sem("bound_ready"), sem("probs_ready"), sem("inv_ready"),
            sem("scaled_ready"), sem("turned_done"),
            sem("probsT_ready"))
        pv_done, attnT_ready, o_done = sem("pv_done"), sem("attnT_ready"), sem("o_done")
        x1_summed, x1_ready = sem("x1_summed"), sem("x1_ready")
        guessed, newton = sem("guessed"), sem("newton")
        offset_mult, offset_ready, offset_here = sem("offset_mult"), sem("offset_ready"), sem("offset_here")
        rooted = sem("rooted")
        vT_done, vT_ready, gated_ready, blocks_done, direct_ready, base_ready = (
            sem("vT_done"), sem("vT_ready"), sem("gated_ready"), sem("blocks_done"), sem("direct_ready"),
            sem("base_ready"))
        kv_ready, conv_done, z_ready, mixT_ready = sem("kv_ready"), sem("conv_done"), sem("z_ready"), sem("mixT_ready")
        mix_done, x2_summed, x2_ready = sem("mix_done"), sem("x2_summed"), sem("x2_ready")
        x2T_done, x2T_ready, gate_done, gating, gate_exp = (
            sem("x2T_done"), sem("x2T_ready"), sem("gate_done"),
            sem("gating"), sem("gate_exp"))
        w_hi_ready, w_lo_ready, x2T_split, h_split, skip_ready = (
            sem("w_hi_ready"), sem("w_lo_ready"), sem("x2T_split"), sem("h_split"), sem("skip_ready"))
        h_done, h_ready, expert_done, combined = sem("h_done"), sem("h_ready"), sem("expert_done"), sem("combined")
        final_ready = sem("final_ready")

        def half(n):
            return slice(HB * n, HB * n + HB)

        def w1(t, c, e):
            return t[:, c * E * HID + e * HID:c * E * HID + (e + 1) * HID]

        def w2(t, e):
            return t[:, C * E * HID + e * D:C * E * HID + (e + 1) * D]

        block = stack.enter_context(nc.Block())

        @block.sync
        def _(sp):
            sp.dma_start(loraB_sb, loraB).then_inc(ld_lora, 16)
            sp.dma_start(loraA_sb, loraA).then_inc(ld_lora, 16)
            sp.dma_start(w_sb[:, Q:V], WT[:, Q:V]).then_inc(ld_w[0], 16)
            sp.dma_start(xT_sb[:, 0], xT[0]).then_inc(ld_xT[0], 16)
            sp.dma_start(w_sb[:, V:], WT[:, V:]).then_inc(ld_w[1], 16)
            sp.dma_start(xT_sb[:, 1], xT[1]).then_inc(ld_xT[1], 16)
            sp.dma_start(ctx_r[:], ctx_rows.rearrange("b s d -> s b d")).then_inc(ld_ctx_rows, 16)
            sp.dma_start(x_sb[:], x.rearrange("b s d -> s b d")).then_inc(ld_x, 16)
            sp.dma_start(ctx_c[:], ctx_cols).then_inc(ld_ctx_cols, 16)
            for u in range(TOEP_SLOTS):
                sp.dma_start(toep_sb[:, u], toep[u]).then_inc(ld_toep[u], 16)
            sp.dma_start(wg_sb[:], wgT).then_inc(ld_wg, 16)
            sp.dma_start(ffn_sb[:], ffnT[:, 0:FFN_W // 2]).then_inc(ld_ffn, 16)
            with sp.Fori(2, B - 1, 2) as i:
                for slot in range(2):
                    sp.wait_ge(v_done, i + slot - 1)
                    sp.dma_start(xT_sb[:, slot], xT[bass.ds(i + slot, 1)].rearrange("o p c s -> (o p) c s")
                                 ).then_inc(ld_xT[slot], 16)
            sp.wait_ge(w_lo_ready, W_PARTS // 2)
            sp.dma_start(ffn_sb[:], ffnT[:, FFN_W // 2:]).then_inc(ld_ffn, 16)
            for n in range(HALVES):
                with sp.Fori(TOEP_SLOTS if n == 0 else 0, NH - TOEP_SLOTS + 1, TOEP_SLOTS) as i:
                    for u in range(TOEP_SLOTS):
                        sp.wait_ge(conv_done, NH * n + i + u - TOEP_SLOTS + 1)
                        sp.dma_start(toep_sb[:, u], toep[bass.ds(i + u, 1)].rearrange("o p k m -> (o p) k m")
                                     ).then_inc(ld_toep[u], 16)
            with sp.Fori(0, B) as b:
                sp.wait_ge(final_ready, b + 1)
                sp.dma_start(out[bass.ds(b, 1)].rearrange("o s d -> (o s) d"),
                             final[:, bass.ds(b, 1), :].rearrange("s o d -> s (o d)")).then_inc(stored, 16)
            sp.wait_ge(stored, 16 * B)

        @block.scalar
        def _(act):
            act.dma_start(const_sb[:], consts).then_inc(ld_const, 16)
            act.dma_start(bqk_sb[:], bqk).then_inc(ld_small, 16)
            act.dma_start(bvo_sb[:], bvo.partition_broadcast(128)).then_inc(ld_small, 16)
            act.dma_start(skip_sb[:], skip_bias).then_inc(ld_small, 16)

            def qk_out(b, slot):
                act.wait_ge(qk_done, b + 1)
                for c in range(C):
                    for m, buf in ((Q, qT), (K, kT)):
                        nc.scalar.activation(buf[:, slot, c], ps_qk[:, (2 * c + m) * S:(2 * c + m + 1) * S],
                                             ACT.Identity, bias=bqk_sb[:, m, c:c + 1]).then_inc(qk_ready, 1)

            def exp(G, par, first=False):
                act.wait_ge(bound_ready, G + 1)
                if not first:
                    act.wait_ge(turned_done, G - 1)
                for w in range(GH):
                    ins = nc.scalar.activation(probs[:, par, w * S:(w + 1) * S], ps_scores[par][:, w * S:(w + 1) * S],
                                               ACT.Exp, bias=bound[:, par, w:w + 1], scale=SCALE,
                                               accum_out=prob_sum[:, par, w:w + 1])
                ins.then_inc(probs_ready, 1)

            def turned_out(G, par, first=False):
                act.wait_ge(turned_done, G + 1)
                if not first:
                    act.wait_ge(pv_done, G - 1)
                nc.scalar.copy(probsT[:, par], ps_turned[par][:]).then_inc(probsT_ready, 1)

            def vT_out(b):
                act.wait_ge(vT_done, b + 1)
                nc.scalar.copy(vT[:, bass.ds(b, 1)].rearrange("p o c s -> p (o c s)"), ps_v[:, D:2 * D]
                               ).then_inc(vT_ready, 1)

            def weights_hi(part, second):
                nc.scalar.copy(ffn_hi[:, bass.ds(W_PART * part, W_PART)],
                               ffn_sb[:, bass.ds(W_PART * (part - W_PARTS // 2 * second), W_PART)]).then_inc(w_hi_ready, 1)

            def step(b, slot, before=2, last=False, part=None):
                for g in range(GROUPS):
                    G = GROUPS * b + g
                    if not last or g < GROUPS - 1:
                        exp(G + 1, (g + 1) % 2, before == 0 and g == 0)
                    if g == 0 and not last:
                        if before:
                            act.wait_ge(scores_done, GROUPS * b)
                            act.wait_ge(kM_ready, 4 * b)
                        qk_out(b + 1, 1 - slot)
                    if g == GROUPS - 1 and before == 2:
                        vT_out(b - 2)
                    turned_out(G, g % 2, before == 0 and g < 2)
                    if g == 2 and part is not None:
                        weights_hi(part, 0)

            act.wait_ge(warm_ready, 1)
            nc.scalar.activation(warmed[:], warm[:, 0:1], ACT.Exp)
            act.wait_ge(ld_small, 48)
            qk_out(0, 0)
            act.wait_ge(ld_ctx_rows, 16)
            nc.scalar.activation(skip_ctx[:].rearrange("p b d -> p (b d)"), ctx_r[:].rearrange("p b d -> p (b d)"),
                                 ACT.Copy, scale=skip_sb[:, 0:1]).then_inc(skip_ready, 1)
            exp(0, 0, True)
            step(0, 0, before=0)
            step(1, 1, before=1)
            act.wait_ge(ld_ffn, 16)
            with act.Fori(2, B - 3, 2) as i:
                step(i, 0, part=i - 2)
                step(i + 1, 1, part=i - 1)
            step(B - 2, 0)
            step(B - 1, 1, last=True)
            vT_out(B - 2)
            act.wait_ge(ld_ffn, 32)
            weights_hi(W_PARTS // 2, 1)
            vT_out(B - 1)
            for part in range(W_PARTS // 2 + 1, W_PARTS):
                weights_hi(part, 1)

            def x2_norm(n):
                act.wait_ge(offset_ready if n == 0 else offset_here, 1)
                for q in range(HB):
                    nc.scalar.activation(x2[:, HB * n + q], x2[:, HB * n + q], ACT.Identity, bias=offset[:, q:q + 1],
                                         scale=rstd[:, q:q + 1]).then_inc(x2_ready, 1)

            def x2T_out(n):
                for t in (x2T, x2T_hi):
                    for q in range(2):
                        pair = 2 * n + q
                        act.wait_ge(x2T_done, pair + 1)
                        nc.scalar.copy(t[:].rearrange("p c (b s) -> p c b s", b=B)[:, :, 2 * pair:2 * pair + 2, :],
                                       ps_turn[q][:].rearrange("p (b c s) -> p c b s", b=2, c=C)).then_inc(x2T_ready, 1)

            def gate_exponent(n):
                act.wait_ge(gating, GATING_OPS * n + GATE_SHIFTED)
                nc.scalar.activation(soft[:, half(n)], soft[:, half(n)], ACT.Exp).then_inc(gate_exp, 1)

            def relu(k, e, first=False):
                act.wait_ge(h_done, k + 1)
                if not first:
                    act.wait_ge(h_split, k - HID_BUFS + 1)
                    act.wait_ge(expert_done, k - HID_BUFS + 1)
                for t in (hT, hT_hi):
                    nc.scalar.activation(t[:, e % HID_BUFS], ps_hidden[e % 2][:, 0:2 * S], ACT.Relu).then_inc(h_ready, 1)

            x2_norm(0)
            x2T_out(0)
            for e in range(E):
                relu(e, e, e < HID_BUFS)
                if e == 1:
                    gate_exponent(0)
            relu(E, 0)
            relu(E + 1, 1)
            x2_norm(1)
            relu(E + 2, 2)
            x2T_out(1)
            relu(E + 3, 3)
            gate_exponent(1)
            with act.Fori(1, B // 2 - 1) as p:
                for e in range(4, E + 4):
                    relu(E * p + e, e % E)
            for e in range(4, E):
                relu(E * (B // 2 - 1) + e, e)

        @block.gpsimd
        def _(pool):
            nc.gpsimd.memset(vz[:], 0.0).then_inc(cleared, 1)
            nc.gpsimd.memset(minus_half[:], -0.5).then_inc(cleared, 1)
            nc.gpsimd.memset(three_halves[:], 1.5).then_inc(cleared, 1)
            nc.gpsimd.memset(minus_one[:], -1.0).then_inc(cleared, 1)

            def mask_keys(b, slot):
                for c in range(C):
                    pool.wait_ge(qk_ready, 4 * b + 2 * c + 2)
                    for e in range(2):
                        nc.gpsimd.tensor_tensor(
                            kM[:, slot, c, e], kT[:, slot, c].unsqueeze(1).to_broadcast([128, GH, S]),
                            head_mask[:, e].unsqueeze(2).to_broadcast([128, GH, S]), ALU.mult).then_inc(kM_ready, 1)

            def inverse_root(call, n, steps=range(NEWTON)):
                done = NEWTON_OPS * call
                v, hv, a, y = nw_v[:, 0:n], nw_h[:, 0:n], nw_a[:, 0:n], rstd[:, 0:n]
                if 0 in steps:
                    pool.wait_ge(guessed, call + 1)
                    nc.gpsimd.tensor_tensor(hv, v, minus_half[:, 0:n], ALU.mult).then_inc(newton, 1)
                for k in steps:
                    at = done + 1 + 4 * k
                    pool.wait_ge(newton, at)
                    nc.gpsimd.tensor_tensor(a, y, y, ALU.mult).then_inc(newton, 1)
                    pool.wait_ge(newton, at + 1)
                    nc.gpsimd.tensor_tensor(a, a, hv, ALU.mult).then_inc(newton, 1)
                    pool.wait_ge(newton, at + 2)
                    nc.gpsimd.tensor_tensor(a, a, three_halves[:, 0:n], ALU.add).then_inc(newton, 1)
                    pool.wait_ge(newton, at + 3)
                    nc.gpsimd.tensor_tensor(y, y, a, ALU.mult).then_inc(newton, 1)

            def row_offset(call):
                pool.wait_ge(newton, NEWTON_OPS * (call + 1))
                nc.gpsimd.tensor_tensor(offset[:], moments[:, :, 0], rstd[:], ALU.mult).then_inc(offset_mult, 1)
                pool.wait_ge(offset_mult, 1)
                nc.gpsimd.tensor_tensor(offset[:], offset[:], minus_one[:], ALU.mult).then_inc(offset_ready, 1)

            def base(b, slot):
                pool.wait_ge(direct_ready, b + 1)
                row = x1[:, bass.ds(b, 1), :].rearrange("p o d -> p (o d)")
                nc.gpsimd.tensor_tensor(row, x1_now[:, slot], direct[:, bass.ds(b, 1), :].rearrange("p o d -> p (o d)"),
                                        ALU.add).then_inc(base_ready, 1)

            def products(n, h, slot, first=False):
                k = NH * n + h
                if not first:
                    pool.wait_ge(conv_done, k - CONV_BUFS + 1)
                shape = [128, HB * C, CH, CH]
                at = lambda t: t[:, half(n), :, bass.ds(CH * h, CH)].rearrange("p b c i -> p (b c) i")
                nc.gpsimd.tensor_tensor(
                    kv[:, slot].rearrange("p (m i j) -> p m i j", i=CH, j=CH), at(vT).unsqueeze(3).to_broadcast(shape),
                    at(ctx_c).unsqueeze(2).to_broadcast(shape), ALU.mult).then_inc(kv_ready, 1)

            pool.wait_ge(ld_const, 16)
            mask_keys(0, 0)
            mask_keys(1, 1)

            def with_bias(b):
                one = x_sb[:, bass.ds(b, 1), :].rearrange("p o d -> p (o d)")
                nc.gpsimd.tensor_tensor(one, one, bvo_sb[:, 1], ALU.add).then_inc(xb_ready, 1)

            def gate_direct(b, slot):
                pool.wait_ge(x1_ready, b + 1)
                nc.gpsimd.tensor_tensor(gated[:, bass.ds(b, 1), :].rearrange("p o d -> p (o d)"), x1_now[:, slot],
                                        skip_ctx[:, bass.ds(b, 1), :].rearrange("p o d -> p (o d)"), ALU.mult
                                        ).then_inc(gated_ready, 1)

            def weights_lo(part, second):
                pool.wait_ge(w_hi_ready, part + 1)
                cut = bass.ds(W_PART * part, W_PART)
                whole = ffn_sb[:, bass.ds(W_PART * (part - W_PARTS // 2 * second), W_PART)]
                nc.gpsimd.tensor_tensor(ffn_lo[:, cut], whole, ffn_hi[:, cut].bitcast(F32), ALU.subtract
                                        ).then_inc(w_lo_ready, 1)

            pool.wait_ge(ld_x, 16)
            pool.wait_ge(ld_small, 48)
            with_bias(0)

            pool.wait_ge(cleared, CLEARED)

            def step(b, slot, before=2, last=False, part=None, root=True):
                if not last:
                    pool.wait_ge(scores_done, GROUPS * b)
                    mask_keys(b + 1, 1 - slot)
                if before == 2:
                    gate_direct(b - 2, slot)
                with_bias(b)
                if part is not None:
                    weights_lo(part, 0)
                if before == 2:
                    base(b - 2, slot)
                if root:
                    inverse_root(b - 1, 1)

            step(1, 1, before=1)
            pool.wait_ge(skip_ready, 1)
            with pool.Fori(2, B - 3, 2) as i:
                step(i, 0, part=i - 2)
                step(i + 1, 1, part=i - 1)
            step(B - 2, 0, root=False)
            pool.wait_ge(ld_ctx_cols, 16)
            pool.wait_ge(vT_ready, HB)
            products(0, 0, 0, True)
            products(0, 1, 1, True)
            inverse_root(B - 3, 1)
            products(0, 2, 2, True)
            products(0, 3, 3, True)
            step(B - 1, 1, last=True)
            products(0, 4, 0)
            gate_direct(B - 2, 0)
            products(0, 5, 1)
            inverse_root(B - 1, 1, (0,))
            products(0, 6, 2)
            inverse_root(B - 1, 1, range(1, NEWTON))
            products(0, 7, 3)
            base(B - 2, 0)
            gate_direct(B - 1, 1)
            with pool.Fori(8, NH - 3, CONV_BUFS) as i:
                for u in range(CONV_BUFS):
                    products(0, i + u, u)
            base(B - 1, 1)
            pool.wait_ge(vT_ready, B)
            with pool.Fori(0, NH // CONV_BUFS - 1) as i:
                for u in range(CONV_BUFS):
                    products(1, CONV_BUFS * i + u, u)
                weights_lo(i + W_PARTS // 2, 1)
            inverse_root(B, HB)
            row_offset(B)
            for u in range(CONV_BUFS):
                products(1, NH - CONV_BUFS + u, u)
            weights_lo(W_PARTS - 1, 1)

            def split_x2T(pair):
                pool.wait_ge(x2T_ready, 4 * (pair // 2) + 3 + pair % 2)
                at = lambda t: t[:, :, 2 * S * pair:2 * S * (pair + 1)]
                nc.gpsimd.tensor_tensor(at(x2T_lo), at(x2T), at(x2T_hi).bitcast(F32), ALU.subtract).then_inc(x2T_split, 1)

            def split_hidden(k, e, first=False):
                pool.wait_ge(h_ready, 2 * k + 2)
                if not first:
                    pool.wait_ge(expert_done, k - HID_BUFS + 1)
                u = e % HID_BUFS
                nc.gpsimd.tensor_tensor(hT_lo[:, u], hT[:, u], hT_hi[:, u].bitcast(F32), ALU.subtract).then_inc(h_split, 1)

            split_x2T(0)
            split_x2T(1)
            for e in range(E):
                split_hidden(e, e, e < HID_BUFS)
            split_hidden(E, 0)
            split_hidden(E + 1, 1)
            split_x2T(2)
            split_hidden(E + 2, 2)
            split_x2T(3)
            split_hidden(E + 3, 3)

            with pool.Fori(1, B // 2 - 1) as p:
                for e in range(4, E + 4):
                    split_hidden(E * p + e, e % E)
                    if e in ROOT_AT:
                        inverse_root(B + p, 2, (ROOT_AT.index(e),))
            for e in range(4, E):
                split_hidden(E * (B // 2 - 1) + e, e)
            inverse_root(B + B // 2 - 1, 2)

        @block.vector
        def _(dve):
            def row(t, b):
                return t[:, bass.ds(b, 1), :].rearrange("p o d -> p (o d)")

            def statistics(rows, here=False, at=0):
                n = len(rows)
                cols = slice(at, at + n)
                dve.drain()
                for u, r in enumerate(rows):
                    nc.vector.bn_stats(stats[:, at + u], r)
                dve.drain()
                for u in range(n):
                    nc.vector.bn_aggr(moments[:, at + u], stats[:, at + u])
                dve.drain()
                v, y = nw_v[:, cols], rstd[:, cols]
                nc.vector.tensor_scalar(v, moments[:, cols, 1], EPS, None, ALU.add)
                if here:
                    nc.vector.tensor_scalar(nw_h[:, cols], moments[:, cols, 1], EPS, -0.5, ALU.add, ALU.mult)
                dve.drain()
                first_guess = nc.vector.tensor_scalar(y.bitcast(I32), v.bitcast(I32), -0.5, float(0x5F3759DF), ALU.mult,
                                                      ALU.add)
                if not here:
                    first_guess.then_inc(guessed, 1)

            rooting = [0]

            def root_here(n, at=0, meanwhile=None):
                def link(ins):
                    rooting[0] += 1
                    ins.then_inc(rooted, 1)
                    if meanwhile and rooting[0] % (3 * NEWTON) == 1:
                        meanwhile()
                    dve.wait_ge(rooted, rooting[0])

                hv, a, y = nw_h[:, at:at + n], nw_a[:, at:at + n], rstd[:, at:at + n]
                dve.drain()
                for _ in range(NEWTON):
                    link(nc.vector.tensor_tensor(a, y, y, ALU.mult))
                    link(nc.vector.tensor_tensor(a, a, hv, ALU.mult))
                    link(nc.vector.scalar_tensor_tensor(out=y, in0=a, scalar=1.5, in1=y, op0=ALU.add, op1=ALU.mult))

            def layernorm(call, rows, outs, ready, at=0):
                if call is not None:
                    dve.wait_ge(newton, NEWTON_OPS * (call + 1))
                for u, (r, o) in enumerate(zip(rows, outs)):
                    nc.vector.tensor_scalar(o, r, moments[:, at + u, 0:1], rstd[:, at + u:at + u + 1], ALU.subtract,
                                            ALU.mult).then_inc(ready, 1)

            nc.vector.memset(warm[:], 0.0).then_inc(warm_ready, 1)
            def add_lora(m):
                dve.wait_ge(ld_w[m // 2], 16)
                dve.wait_ge(lora_done, m + 1)
                nc.vector.scalar_tensor_tensor(
                    out=w_sb[:, m].rearrange("p c d -> p (c d)"), in0=ps_lora[m][:], scalar=LORA,
                    in1=w_sb[:, m].rearrange("p c d -> p (c d)"), op0=ALU.mult, op1=ALU.add).then_inc(w_ready, 1)

            def v_out(b, slot):
                dve.wait_ge(v_done, b + 1)
                for e in range(2):
                    cut = lambda t: t.rearrange("p (c w e d) -> p c w e d", c=C, w=GH, e=2)[:, :, :, e, :]
                    nc.vector.tensor_tensor(vz[:, slot, :, e, :, HD * e:HD * (e + 1)], cut(ps_v[:, 0:D]),
                                            cut(bvo_sb[:, 0]), ALU.add).then_inc(v_ready, 1)

            def row_bound(G, par, first=False):
                dve.wait_ge(scores_done, G + 1)
                nc.vector.tensor_reduce(rowmax[:, par], ps_scores[par][:].rearrange("p (h k) -> p h k", h=GH), AX.X,
                                        ALU.max).then_inc(max_ready, 1)
                if not first:
                    dve.wait_ge(probs_ready, G - 1)
                dve.wait_ge(max_ready, G + 1)
                nc.vector.tensor_scalar(bound[:, par], rowmax[:, par], -SCALE, None, ALU.mult).then_inc(bound_ready, 1)

            def scale(G, par):
                dve.wait_ge(probs_ready, G + 1)
                nc.vector.reciprocal(inv_sum[:, par], prob_sum[:, par]).then_inc(inv_ready, 1)
                dve.wait_ge(inv_ready, G + 1)
                heads = probs[:, par].rearrange("p (h k) -> p h k", h=GH)
                nc.vector.tensor_tensor(heads, heads, inv_sum[:, par].unsqueeze(2).to_broadcast([S, GH, S]), ALU.mult
                                        ).then_inc(scaled_ready, 1)

            def attn_out(b):
                dve.wait_ge(pv_done, GROUPS * b + GROUPS)
                nc.vector.tensor_copy(attnT[:].rearrange("p c s -> p (c s)"), ps_attn[:, 0:D]).then_inc(attnT_ready, 1)

            def residual(b):
                dve.wait_ge(o_done, b + 1)
                nc.vector.tensor_tensor(row(x1, b), ps_o[:, 0:D], row(x_sb, b), ALU.add).then_inc(x1_summed, 1)

            def direct_out(b):
                dve.wait_ge(blocks_done, b + 1)
                nc.vector.tensor_tensor(row(direct, b), ps_o[:, D:2 * D], row(ctx_r, b), ALU.mult
                                        ).then_inc(direct_ready, 1)

            def step(b, slot, before=2, last=False):
                for g in range(GROUPS):
                    G = GROUPS * b + g
                    scale(G, g % 2)
                    if g < 2 or not last:
                        row_bound(G + 2, g % 2)
                    if g == 0 and before:
                        attn_out(b - 1)
                    if g == 1 and not last:
                        v_out(b + 1, 1 - slot)
                    if g == 2 and before:
                        dve.wait_ge(xb_ready, b)
                        residual(b - 1)
                    if g == 2 and before == 2:
                        layernorm(b - 2, [row(x1, b - 2)], [x1_now[:, slot]], x1_ready)
                    if g == 3 and before == 2:
                        direct_out(b - 2)
                    if g == 3 and before:
                        statistics([row(x1, b - 1)])

            for m in (Q, K, V):
                add_lora(m)
            row_bound(0, 0, True)
            row_bound(1, 1, True)
            add_lora(O)
            dve.wait_ge(ld_small, 48)
            dve.wait_ge(cleared, CLEARED)
            v_out(0, 0)
            step(0, 0, before=0)
            step(1, 1, before=1)
            dve.wait_ge(ld_ctx_rows, 16)
            dve.wait_ge(ld_ctx_cols, 16)
            with dve.Fori(2, B - 3, 2) as i:
                step(i, 0)
                step(i + 1, 1)
            step(B - 2, 0)
            step(B - 1, 1, last=True)

            def query(n, h, k, par, first=False):
                dve.wait_ge(conv_done, k + 1)
                if not first:
                    dve.wait_ge(mixT_ready, k - 1)
                nc.vector.tensor_tensor(
                    z[:, par % 2].rearrange("p (m i j) -> p m i j", i=CH, j=CH),
                    ps_conv[par][:].rearrange("p (m i j) -> p m i j", i=CH, j=CH),
                    ctx_c[:, half(n), :, bass.ds(CH * h, CH)].rearrange("p b c i -> p (b c) i").unsqueeze(3)
                    .to_broadcast([128, HB * C, CH, CH]), ALU.mult).then_inc(z_ready, 1)

            def gather(n, h, k, par):
                dve.wait_ge(z_ready, k + 1)
                nc.vector.tensor_reduce(
                    mixT[:, half(n), :, bass.ds(CH * h, CH)].rearrange("p b c i -> p (b c) i"),
                    z[:, par % 2].rearrange("p (m i j) -> p m j i", i=CH, j=CH), AX.X, ALU.add).then_inc(mixT_ready, 1)

            def two_heads(n, h, u):
                k = NH * n + h
                first = isinstance(k, int) and k == 0
                query(n, h, k, u, first)
                query(n, h + 1, k + 1, u + 1, first)
                gather(n, h, k, u)
                gather(n, h + 1, k + 1, u + 1)

            attn_out(B - 1)
            two_heads(0, 0, 0)
            layernorm(B - 2, [x1[:, B - 2]], [x1_now[:, 0]], x1_ready)
            dve.wait_ge(xb_ready, B)
            residual(B - 1)
            statistics([x1[:, B - 1]])
            two_heads(0, 2, 2)
            direct_out(B - 2)
            two_heads(0, 4, 0)
            layernorm(B - 1, [x1[:, B - 1]], [x1_now[:, 1]], x1_ready)
            two_heads(0, 6, 2)
            direct_out(B - 1)
            with dve.Fori(2 * CONV_BUFS, NH - 3, CONV_BUFS) as i:
                two_heads(0, i, 0)
                two_heads(0, i + 2, 2)

            def x2_sum(pair):
                dve.wait_ge(mix_done, pair + 1)
                for b in (2 * pair, 2 * pair + 1):
                    dve.wait_ge(base_ready, b + 1)
                    nc.vector.tensor_tensor(x2[:, b], ps_turn[b // 2 % 2][:, (b % 2) * D:(b % 2 + 1) * D], x1[:, b],
                                            ALU.add).then_inc(x2_summed, 1)

            two_heads(1, 0, 0)
            two_heads(1, 2, 2)
            x2_sum(0)
            x2_sum(1)
            statistics([x2[:, b] for b in range(HB)])
            with dve.Fori(CONV_BUFS, NH - 7, CONV_BUFS) as i:
                two_heads(1, i, 0)
                two_heads(1, i + 2, 2)
            two_heads(1, NH - 4, 0)
            two_heads(1, NH - 2, 2)
            full, every_pair = [S, HB, E], [S, HB, E, E]

            def four(t, n):
                return t[:, half(n)].rearrange("p b (e f) -> p b e f", e=E)

            def issue(ins):
                ins.then_inc(gating, 1)

            def settled(n, count):
                dve.wait_ge(gating, GATING_OPS * n + count)

            def gate_order(n):
                h = half(n)
                theirs = gate[:, h].unsqueeze(2).to_broadcast(every_pair)
                own = gate[:, h].unsqueeze(3).to_broadcast(every_pair)
                dve.wait_ge(gate_done, n + 1)
                issue(nc.vector.tensor_copy(gate[:, h].rearrange("p b e -> p (b e)"), ps_gates[n][:, 0:HB * E]))
                settled(n, 1)
                issue(nc.vector.tensor_reduce(top[:, h], gate[:, h], AX.X, ALU.max))
                issue(nc.vector.tensor_tensor(four(above, n), theirs, own, ALU.is_gt))
                settled(n, 2)
                issue(nc.vector.tensor_tensor(soft[:, h], gate[:, h], top[:, h].unsqueeze(2).to_broadcast(full),
                                              ALU.subtract))
                issue(nc.vector.tensor_tensor(four(ties, n), theirs, own, ALU.is_equal))

            def gate_rank(n):
                h = half(n)
                settled(n, 5)
                issue(nc.vector.tensor_tensor(ties[:, h], ties[:, h], earlier.unsqueeze(1).to_broadcast([S, HB, E * E]),
                                              ALU.mult))
                settled(n, 6)
                issue(nc.vector.tensor_tensor(above[:, h], above[:, h], ties[:, h], ALU.add))
                settled(n, 7)
                issue(nc.vector.tensor_reduce(rank[:, h], four(above, n), AX.X, ALU.add))

            def gate_soft(n):
                h = half(n)
                settled(n, 8)
                issue(nc.vector.tensor_scalar(chosen[:, h], rank[:, h], float(TOP), None, ALU.is_lt))
                dve.wait_ge(gate_exp, n + 1)
                issue(nc.vector.scalar_tensor_tensor(out=soft[:, h], in0=rank[:, h], scalar=float(TOP), in1=soft[:, h],
                                                     op0=ALU.is_lt, op1=ALU.mult))
                settled(n, 10)
                issue(nc.vector.tensor_reduce(total[:, h], soft[:, h], AX.X, ALU.add))
                settled(n, 11)
                issue(nc.vector.reciprocal(total[:, h], total[:, h]))

            def gate_weight(n):
                h = half(n)
                settled(n, 12)
                issue(nc.vector.tensor_tensor(soft[:, h], soft[:, h], total[:, h].unsqueeze(2).to_broadcast(full), ALU.mult))
                settled(n, 13)
                issue(nc.vector.scalar_tensor_tensor(out=weight[:, h], in0=soft[:, h], scalar=1.0, in1=soft[:, h],
                                                     op0=ALU.add, op1=ALU.subtract))
                settled(n, 14)
                issue(nc.vector.tensor_tensor(weight[:, h], weight[:, h], chosen[:, h], ALU.mult))
                settled(n, 15)

            def combine(p, e, first=False):
                k = E * p + e
                dve.wait_ge(expert_done, k + 1)
                for u in range(2):
                    if not first:
                        dve.wait_ge(combined, 2 * k + u - 1)
                    nc.vector.scalar_tensor_tensor(
                        out=row(x2, 2 * p + u), in0=ps_expert[e % EXPERT_BUFS][:, u * D:(u + 1) * D],
                        scalar=row(weight, 2 * p + u)[:, e:e + 1], in1=row(x2, 2 * p + u),
                        op0=ALU.mult, op1=ALU.add).then_inc(combined, 1)

            def finish(p, here=False, at=0):
                layernorm(None if here else B + 1 + p, [row(x2, 2 * p + u) for u in range(2)],
                          [row(final, 2 * p + u) for u in range(2)], final_ready, at)

            gate_order(0)
            gate_rank(0)
            gate_soft(0)
            gate_weight(0)
            x2_sum(2)
            x2_sum(3)
            for e in range(E):
                combine(0, e, e == 0)
                if e == 0:
                    statistics([x2[:, b] for b in range(HB, B)], here=True)
                if e == 2:
                    root_here(HB)
                    nc.vector.scalar_tensor_tensor(out=offset[:], in0=moments[:, :, 0], scalar=-1.0, in1=rstd[:],
                                                   op0=ALU.mult, op1=ALU.mult).then_inc(offset_here, 1)
            dve.wait_ge(x2_ready, B)
            statistics([x2[:, 0], x2[:, 1]])
            combine(1, 0)
            combine(1, 1)
            gate_order(1)
            combine(1, 2)
            gate_rank(1)
            combine(1, 3)
            gate_soft(1)
            combine(1, 4)
            gate_weight(1)
            for e in range(5, E):
                combine(1, e)
            with dve.Fori(2, B // 2) as p:
                for e in range(E):
                    combine(p, e)
                    if e == 0:
                        finish(p - 2)
                        statistics([row(x2, 2 * (p - 1)), row(x2, 2 * (p - 1) + 1)])
            statistics([x2[:, B - 2], x2[:, B - 1]], here=True, at=2)
            root_here(2, at=2, meanwhile=lambda: finish(B // 2 - 2))
            finish(B // 2 - 1, here=True, at=2)

        @block.tensor
        def _(pe):
            mm = nc.tensor.matmul
            turn_block = nc.tensor.transpose
            pe.wait_ge(warm_ready, 1)
            for _ in range(WARM):
                mm(bank[0][:, 0:S], warm[:], warm[:], start=True, stop=True)
            pe.wait_ge(ld_lora, 32)

            def lora(m):
                for c in range(C):
                    last = mm(ps_lora[m][:, c * D:(c + 1) * D], loraB_sb[:, m, c * 128:(c + 1) * 128], loraA_sb[:, m],
                              start=True, stop=True)
                last.then_inc(lora_done, 1)

            def project_qk(b, slot, first=False):
                pe.wait_ge(ld_xT[slot], 8 * (b - slot) + 16)
                if not first:
                    pe.wait_ge(qk_ready, 4 * b)
                for c in range(C):
                    for m in (Q, K):
                        at = 2 * c + m
                        for d in range(C):
                            last = mm(ps_qk[:, at * S:(at + 1) * S], w_sb[:, m, d, c * 128:(c + 1) * 128],
                                      xT_sb[:, slot, d], start=(d == 0), stop=(d == C - 1))
                last.then_inc(qk_done, 1)

            def project_v(b, slot, first=False):
                if not first:
                    pe.wait_ge(v_ready, 2 * b)
                for d in range(C):
                    last = mm(ps_v[:, 0:D], xT_sb[:, slot, d], w_sb[:, V, d], start=(d == 0), stop=(d == C - 1))
                last.then_inc(v_done, 1)

            def scores(b, g, slot, first=False):
                c, e = g // 2, g % 2
                if e == 0:
                    pe.wait_ge(qk_ready, 4 * b + 2 * c + 1)
                pe.wait_ge(kM_ready, 4 * b + 2 * c + e + 1)
                if not first:
                    pe.wait_ge(probs_ready, GROUPS * b + g - 1)
                mm(ps_scores[e][:], qT[:, slot, c], kM[:, slot, c, e].rearrange("p w s -> p (w s)"), start=True,
                   stop=True).then_inc(scores_done, 1)

            def turn(G, par, first=False):
                pe.wait_ge(scaled_ready, G + 1)
                if not first:
                    pe.wait_ge(probsT_ready, G - 1)
                for n in range(GH):
                    last = turn_block(ps_turned[par][:, n * S:(n + 1) * S], probs[:, par, n * S:(n + 1) * S], ident)
                last.then_inc(turned_done, 1)

            def weigh(b, g, slot, first=False):
                c, e = g // 2, g % 2
                G = GROUPS * b + g
                pe.wait_ge(probsT_ready, G + 1)
                if g == 0:
                    pe.wait_ge(v_ready, 2 * b + 2)
                    if not first:
                        pe.wait_ge(attnT_ready, b)
                for w in range(GH):
                    last = mm(ps_attn[32 * w:32 * w + 32, c * S:(c + 1) * S], vz[:, slot, c, e, w],
                              probsT[:, e, w * S:(w + 1) * S], start=(g == 0), stop=(g == GROUPS - 1),
                              skip_group_check=True)
                last.then_inc(pv_done, 1)

            def project_o(b):
                pe.wait_ge(attnT_ready, b + 1)
                for c in range(C):
                    last = mm(ps_o[:, 0:D], attnT[:, c], w_sb[:, O, c], start=(c == 0), stop=(c == C - 1))
                last.then_inc(o_done, 1)

            def turn_x1(b, slot, v_before):
                pe.wait_ge(v_ready, 2 * v_before)
                pe.wait_ge(x1_ready, b + 1)
                for c in range(C):
                    last = turn_block(ps_v[:, D + c * 128:D + (c + 1) * 128],
                                      x1_now[:, slot, c * 128:(c + 1) * 128], ident)
                last.then_inc(vT_done, 1)

            def convolve(k, slot, first=False):
                pe.wait_ge(ld_toep[slot], 4 * (k - slot) + 16)
                pe.wait_ge(kv_ready, k + 1)
                if not first:
                    pe.wait_ge(z_ready, k - CONV_BUFS + 1)
                near, far = toep_sb[:, slot, 0], toep_sb[:, slot, 1]
                chunk = lambda t, c: t.rearrange("p (b c n) -> p b c n", b=HB, c=C)[:, :, c]
                mm(ps_conv[slot][:], near, kv[:, slot], start=True, stop=False)
                mm(chunk(ps_conv[slot][:], 1), far, chunk(kv[:, slot], 0), start=False, stop=True).then_inc(conv_done, 1)

            def sum_channels(b, x1_before):
                pe.wait_ge(gated_ready, b + 1)
                pe.wait_ge(x1_summed, x1_before)
                mm(ps_o[:, D:2 * D], block_ones, gated[:, bass.ds(b, 1), :].rearrange("p o d -> p (o d)"),
                   start=True, stop=True).then_inc(blocks_done, 1)

            def step(b, slot, before=2, last=False):
                for g in range(GROUPS):
                    if g < 2:
                        scores(b, g + 2, slot)
                    elif not last:
                        scores(b + 1, g - 2, 1 - slot)
                    if g == 0 and before and not last:
                        project_qk(b + 1, 1 - slot)
                    if g == 1 and not last:
                        project_v(b + 1, 1 - slot)
                    elif g == 1:
                        convolve(0, 0, True)
                    if g == 2 and before:
                        project_o(b - 1)
                    if g == GROUPS - 1 and before == 2:
                        turn_x1(b - 2, slot, B if last else b + 2)
                        sum_channels(b - 2, b)
                    turn(GROUPS * b + g, g % 2, before == 0 and g < 2)
                    if g > 0:
                        weigh(b, g - 1, slot, before == 0)
                    elif before:
                        weigh(b - 1, GROUPS - 1, 1 - slot)
                if before == 2:
                    pe.wait_ge(vT_ready, b - 1)

            for m in (Q, K, V):
                lora(m)
            pe.wait_ge(w_ready, K + 1)
            project_qk(0, 0, True)
            pe.wait_ge(w_ready, V + 1)
            project_v(0, 0, True)
            lora(O)
            pe.wait_ge(ld_const, 16)
            pe.wait_ge(cleared, CLEARED)
            scores(0, 0, 0, True)
            scores(0, 1, 0, True)
            project_qk(1, 1)
            step(0, 0, before=0)
            step(1, 1, before=1)
            with pe.Fori(2, B - 3, 2) as i:
                step(i, 0)
                step(i + 1, 1)
            step(B - 2, 0)
            step(B - 1, 1, last=True)
            weigh(B - 1, GROUPS - 1, 1)

            convolve(1, 1, True)
            project_o(B - 1)
            convolve(2, 2, True)
            turn_x1(B - 2, 0, B)
            convolve(3, 3, True)
            sum_channels(B - 2, B)
            convolve(4, 0)
            convolve(5, 1)
            convolve(6, 2)
            pe.wait_ge(vT_ready, B - 1)
            turn_x1(B - 1, 1, B)
            convolve(7, 3)
            pe.wait_ge(direct_ready, B - 1)
            sum_channels(B - 1, B)
            with pe.Fori(2 * CONV_BUFS, NH - 3, CONV_BUFS) as i:
                for u in range(CONV_BUFS):
                    convolve(i + u, u)

            def turn_mix(pair):
                for b in (2 * pair, 2 * pair + 1):
                    for c in range(C):
                        at = (b % 2) * D + c * 128
                        last = turn_block(ps_turn[b // 2 % 2][:, at:at + 128], mixT[:, b, c], ident)
                last.then_inc(mix_done, 1)

            def turn_x2(n):
                for b in range(HB * n, HB * n + HB):
                    pe.wait_ge(x2_ready, b + 1)
                    for c in range(C):
                        at = (b % 2) * D + c * 128
                        last = turn_block(ps_turn[b // 2 % 2][:, at:at + 128], x2[:, b, c * 128:(c + 1) * 128], ident)
                    if b % 2:
                        last.then_inc(x2T_done, 1)

            def gate_rows(n):
                pe.wait_ge(x2T_ready, 4 * n + 3)
                for q in range(HB):
                    b = HB * n + q
                    for c in range(C):
                        last = mm(ps_gates[n][:, q * E:(q + 1) * E], x2T[:, c, b * S:(b + 1) * S], wg_sb[:, c],
                                  start=(c == 0), stop=(c == C - 1))
                last.then_inc(gate_done, 1)

            for u in range(CONV_BUFS):
                convolve(NH + u, u)
            pe.wait_ge(mixT_ready, NH)
            pe.wait_ge(vT_ready, B)
            pe.wait_ge(direct_ready, B)
            turn_mix(0)
            turn_mix(1)
            with pe.Fori(CONV_BUFS, NH - 7, CONV_BUFS) as i:
                for u in range(CONV_BUFS):
                    convolve(NH + i + u, u)
            for u in range(CONV_BUFS):
                convolve(2 * NH - CONV_BUFS + u, u)
                if u == 1:
                    turn_x2(0)

            def passes(out, hi, lo, rhs_hi, rhs_lo, start, stop):
                mm(out, lo, rhs_hi, start=start, stop=False)
                mm(out, hi, rhs_lo, start=False, stop=False)
                return mm(out, hi, rhs_hi, start=False, stop=stop)

            def hidden(p, e, first=False):
                k = E * p + e
                if e == 0:
                    pe.wait_ge(x2T_split, p + 1)
                if not first:
                    pe.wait_ge(h_ready, 2 * k - 2)
                for c in range(C):
                    at = lambda t: t[:, c, bass.ds(2 * S * p, 2 * S)]
                    last = passes(ps_hidden[e % 2][:, 0:2 * S], w1(ffn_hi, c, e), w1(ffn_lo, c, e), at(x2T_hi), at(x2T_lo),
                                  c == 0, c == C - 1)
                last.then_inc(h_done, 1)

            def expert(p, e, first=False):
                k = E * p + e
                pe.wait_ge(h_split, k + 1)
                if not first:
                    pe.wait_ge(combined, 2 * (k - EXPERT_BUFS) + 2)
                for u in range(2):
                    at = lambda t: t[:, e % HID_BUFS, u * S:(u + 1) * S]
                    last = passes(ps_expert[e % EXPERT_BUFS][:, u * D:(u + 1) * D], at(hT_hi), at(hT_lo), w2(ffn_hi, e),
                                  w2(ffn_lo, e), True, True)
                last.then_inc(expert_done, 1)

            pe.wait_ge(ld_wg, 16)
            pe.wait_ge(z_ready, 2 * NH - CONV_BUFS + 1)
            gate_rows(0)
            pe.wait_ge(w_lo_ready, W_PARTS)
            hidden(0, 0, True)
            hidden(0, 1, True)
            pe.wait_ge(mixT_ready, 2 * NH)
            pe.wait_ge(x2T_ready, 4)
            turn_mix(B // 4)
            turn_mix(B // 4 + 1)
            pe.wait_ge(z_ready, 2 * NH)

            def hidden_and_expert(p, e, first=False, last=False):
                if not last or e + AHEAD < E:
                    hidden(p + (e + AHEAD) // E, (e + AHEAD) % E)
                expert(p + e // E, e % E, first)

            for e in range(E + 2):
                if e == 3:
                    pe.wait_ge(gating, 1)
                hidden_and_expert(0, e, e < EXPERT_BUFS)
                if e == 8:
                    turn_x2(1)
                if e == 9:
                    gate_rows(1)
            with pe.Fori(1, B // 2 - 1) as p:
                for e in range(2, E + 2):
                    hidden_and_expert(p, e)
            for e in range(2, E):
                hidden_and_expert(B // 2 - 1, e, last=True)


CLEARED = 4
GATE_SHIFTED = 4
GATING_OPS = 15


INS = ["x", "xT", "ctx_rows", "ctx_cols", "WT", "loraB", "loraA", "bqk", "bvo", "skip_bias", "toep", "ffnT", "wgT",
       "consts"]


def kernel(**inputs):
    import numpy as np
    import concourse.bacc as bacc
    from concourse.bass_utils import run_bass_kernel_spmd

    a = {k: np.asarray(v) for k, v in inputs.items()}
    x, ctx = a["x"], a["ctx_2048"]
    names = "qkvo"
    chunked = lambda t: t.reshape(C, 128, -1).transpose(1, 0, 2)
    k = a["L0_xattn_k"]
    padded = np.zeros((NH, 128 + D), k.dtype)
    padded[:, 128:] = k
    m, l = np.arange(128)[:, None], np.arange(128)[None, :]
    toep = np.stack([padded[:, 128 + 128 * part + l - m] for part in range(2)], axis=2)
    consts = np.zeros((128, CONSTS), np.float32)
    p = np.arange(128)
    consts[p, IDENT + p] = 1
    consts[:, BLOCK:BLOCK + 128] = p[:, None] // CH == p[None, :] // CH
    for e in range(2):
        for w in range(GH):
            consts[:, HMASK + GH * e + w] = p // HD == 2 * w + e
    ex = np.arange(E)
    consts[:, TRI:TRI + E * E] = (ex[None, :] < ex[:, None]).reshape(-1)[None, :]
    arrays = {
        "x": x,
        "xT": x.reshape(B, S, C, 128).transpose(0, 3, 2, 1),
        "ctx_rows": ctx,
        "ctx_cols": ctx.reshape(B, S, C, 128).transpose(3, 0, 2, 1),
        "WT": np.stack([chunked(a[f"L0_attn_W{n}"].T) for n in names], axis=1),
        "loraB": np.stack([a[f"L0_attn_B{n}"] for n in names], axis=1),
        "loraA": np.stack([a[f"L0_attn_A{n}"].T for n in names], axis=1),
        "bqk": np.stack([a[f"L0_attn_b{n}"].reshape(C, 128).T for n in "qk"], axis=1),
        "bvo": np.stack([a[f"L0_attn_b{n}"] for n in "vo"], axis=0),
        "skip_bias": a["fside_S2_0"].reshape(S, 1),
        "toep": toep,
        "ffnT": np.concatenate([chunked(a["L0_ffn_w1"].transpose(2, 0, 1).reshape(D, E * HID)).reshape(128, -1),
                                a["L0_ffn_w2"].transpose(2, 0, 1).reshape(HID, -1)], axis=1),
        "wgT": chunked(a["L0_ffn_wg"]),
        "consts": consts,
    }
    arrays = {f"in_{n}": np.ascontiguousarray(v) for n, v in arrays.items()}
    nc = bacc.Bacc("TRN2", target_bir_lowering=False, num_devices=1)
    args = [nc.dram_tensor(f"in_{n}", arrays[f"in_{n}"].shape, mybir.dt.from_np(arrays[f"in_{n}"].dtype),
                           kind="ExternalInput").ap() for n in INS]
    out = nc.dram_tensor("out", (B, S, D), F32, kind="ExternalOutput").ap()
    program(nc, *args, out)
    r = run_bass_kernel_spmd(nc, [arrays], core_ids=[0])
    return r.results[0]["out"]
```
